# Optimizing a Trainium2 kernel written in Bass

```python
import numpy as np
import jax
import jax.numpy as jnp

def _softmax(x, axis=-1):
    return jax.nn.softmax(x, axis=axis)

def _gelu(x):
    return jax.nn.gelu(x, approximate=True)

def _silu(x):
    return jax.nn.silu(x)

def _sigmoid(x):
    return jax.nn.sigmoid(x)

def _layernorm(x, axis=-1, eps=1e-05):
    m = jnp.mean(x, axis=axis, keepdims=True)
    v = jnp.var(x, axis=axis, keepdims=True)
    return (x - m) / jnp.sqrt(v + eps)

def _scatter_add(tgt, idx, src, axis=0):
    return tgt.at[idx].add(src)

def _segment_sum(src, seg, n):
    return jax.ops.segment_sum(src, seg, n)
kernel_name = 'mk_vit_tower_d1_tok_img1024_r4_ebd50e'

def setup_inputs(seed: int=0):
    np.random.seed(seed)
    _w = jnp.asarray

    def _rec_inputs():
        import jax
        import jax.numpy as jnp
        _rk = jax.random.key(seed)
        x = jax.random.uniform(jax.random.fold_in(_rk, 1), (64, 3, 256, 256), jnp.float32, 0.0, 1)
        return x
    x = _rec_inputs()

    def _L0_tok_setup():
        import jax, jax.numpy as jnp
        import numpy as np
        _GRAY_W = (0.2989, 0.587, 0.114)
        key = jax.random.key(seed)
        x = jax.random.uniform(key, (32, 3, 256, 256), dtype=jnp.float32)
        sx = jnp.array([[-3.0, 0.0, 3.0], [-10.0, 0.0, 10.0], [-3.0, 0.0, 3.0]], dtype=jnp.float32)
        scharr = jnp.stack([sx, sx.T])[:, None, :, :]
        return {'x': x, 'scharr': scharr}
    _L0_tok_all = _L0_tok_setup()
    _L0_tok_in = {k: v for k, v in _L0_tok_all.items() if k in ('scharr',)}
    del _L0_tok_all

    def _L0_attn_setup():
        import jax, jax.numpy as jnp
        import numpy as np
        import math
        D_MODEL = 256
        LAYER_ID = 6
        NUM_LAYERS = 12
        B = 8
        T = 512

        def _wkv(w, u, k, v):
            wn = -jnp.exp(w)

            def step(carry, kv):
                aa, bb, pp = carry
                kt, vt = kv
                ww = u + kt
                p = jnp.maximum(pp, ww)
                e1 = jnp.exp(pp - p)
                e2 = jnp.exp(ww - p)
                y = (e1 * aa + e2 * vt) / (e1 * bb + e2)
                ww2 = pp + wn
                p2 = jnp.maximum(ww2, kt)
                e1b = jnp.exp(ww2 - p2)
                e2b = jnp.exp(kt - p2)
                return ((e1b * aa + e2b * vt, e1b * bb + e2b, p2), y)
            Bd, Td, Cd = k.shape
            init = (jnp.zeros((Bd, Cd), k.dtype), jnp.zeros((Bd, Cd), k.dtype), jnp.full((Bd, Cd), -1e+38, k.dtype))
            kT = jnp.swapaxes(k, 0, 1)
            vT = jnp.swapaxes(v, 0, 1)
            _, ys = jax.lax.scan(step, init, (kT, vT))
            return jnp.swapaxes(ys, 0, 1)
        key = jax.random.key(seed)
        ks = jax.random.split(key, 5)
        r01 = LAYER_ID / (NUM_LAYERS - 1)
        r1a0 = 1.0 - LAYER_ID / NUM_LAYERS
        h = np.arange(D_MODEL, dtype=np.float32)
        w = (-5.0 + 8.0 * (h / (D_MODEL - 1)) ** (0.7 + 1.3 * r01)).astype(np.float32)
        zigzag = np.array([(i + 1) % 3 - 1 for i in range(D_MODEL)], np.float32) * 0.5
        u = (np.ones(D_MODEL, np.float32) * math.log(0.3) + zigzag).astype(np.float32)
        xinit = (h / D_MODEL).astype(np.float32)
        tmk = (xinit ** r1a0).reshape(1, 1, D_MODEL).astype(np.float32)
        tmv = (tmk + 0.3 * r01).astype(np.float32)
        tmr = (xinit ** (0.5 * r1a0)).reshape(1, 1, D_MODEL).astype(np.float32)
        s = 1.0 / math.sqrt(D_MODEL)
        Wk = jax.random.normal(ks[0], (D_MODEL, D_MODEL), jnp.float32) * s
        Wv = jax.random.normal(ks[1], (D_MODEL, D_MODEL), jnp.float32) * s
        Wr = jax.random.normal(ks[2], (D_MODEL, D_MODEL), jnp.float32) * s
        Wo = jax.random.normal(ks[3], (D_MODEL, D_MODEL), jnp.float32) * s
        x = jax.random.normal(ks[4], (B, T, D_MODEL), jnp.float32)
        return dict(x=x, w=jnp.asarray(w), u=jnp.asarray(u), time_mix_k=jnp.asarray(tmk), time_mix_v=jnpp if False else jnp.asarray(tmv), time_mix_r=jnp.asarray(tmr), Wk=Wk, Wv=Wv, Wr=Wr, Wo=Wo)
    _L0_attn_all = _L0_attn_setup()
    _L0_attn_in = {k: v for k, v in _L0_attn_all.items() if k in ('w', 'u', 'time_mix_k', 'time_mix_v', 'time_mix_r', 'Wk', 'Wv', 'Wr', 'Wo')}
    del _L0_attn_all

    def _L0_ffn_setup():
        import jax, jax.numpy as jnp
        import numpy as np
        B, T, D, E, H = (8, 512, 256, 8, 64)
        LN_EPS = 1e-05
        key = jax.random.key(seed)
        ks = jax.random.split(key, 4)
        return {'x': jax.random.normal(ks[0], (B, T, D), dtype=jnp.float32), 'Wg': jax.random.normal(ks[1], (E, D), dtype=jnp.float32) * 0.02, 'ln_scale': jnp.ones((E, D), dtype=jnp.float32), 'ln_bias': jnp.zeros((E, D), dtype=jnp.float32), 'W1': jax.random.normal(ks[2], (E, D, H), dtype=jnp.float32) * 0.02, 'b1': jnp.zeros((E, H), dtype=jnp.float32), 'W2': jax.random.normal(ks[3], (E, H, D), dtype=jnp.float32) * 0.02, 'b2': jnp.zeros((E, D), dtype=jnp.float32)}
    _L0_ffn_all = _L0_ffn_setup()
    _L0_ffn_in = {k: v for k, v in _L0_ffn_all.items() if k in ('Wg', 'ln_scale', 'ln_bias', 'W1', 'b1', 'W2', 'b2')}
    del _L0_ffn_all
    return {'x': x, 'L0_tok_scharr': _L0_tok_in['scharr'], 'L0_attn_w': _L0_attn_in['w'], 'L0_attn_u': _L0_attn_in['u'], 'L0_attn_time_mix_k': _L0_attn_in['time_mix_k'], 'L0_attn_time_mix_v': _L0_attn_in['time_mix_v'], 'L0_attn_time_mix_r': _L0_attn_in['time_mix_r'], 'L0_attn_Wk': _L0_attn_in['Wk'], 'L0_attn_Wv': _L0_attn_in['Wv'], 'L0_attn_Wr': _L0_attn_in['Wr'], 'L0_attn_Wo': _L0_attn_in['Wo'], 'L0_ffn_Wg': _L0_ffn_in['Wg'], 'L0_ffn_ln_scale': _L0_ffn_in['ln_scale'], 'L0_ffn_ln_bias': _L0_ffn_in['ln_bias'], 'L0_ffn_W1': _L0_ffn_in['W1'], 'L0_ffn_b1': _L0_ffn_in['b1'], 'L0_ffn_W2': _L0_ffn_in['W2'], 'L0_ffn_b2': _L0_ffn_in['b2']}

def reference(x, L0_tok_scharr, L0_attn_w, L0_attn_u, L0_attn_time_mix_k, L0_attn_time_mix_v, L0_attn_time_mix_r, L0_attn_Wk, L0_attn_Wv, L0_attn_Wr, L0_attn_Wo, L0_ffn_Wg, L0_ffn_ln_scale, L0_ffn_ln_bias, L0_ffn_W1, L0_ffn_b1, L0_ffn_W2, L0_ffn_b2):
    import jax
    import jax.numpy as jnp

    def _L0_tok_ref(x, scharr):
        import jax, jax.numpy as jnp
        import numpy as np
        _GRAY_W = (0.2989, 0.587, 0.114)
        w = jnp.asarray(_GRAY_W, dtype=x.dtype)
        gray = jnp.einsum('bchw,c->bhw', x, w)[:, None]
        edges = jax.lax.conv_general_dilated(gray, scharr, window_strides=(1, 1), padding='SAME', dimension_numbers=('NCHW', 'OIHW', 'NCHW'))
        abs_edges = jnp.sqrt(jnp.square(edges))
        edge = abs_edges.sum(axis=1) / 2
        return edge

    def _L0_attn_ref(x, w, u, time_mix_k, time_mix_v, time_mix_r, Wk, Wv, Wr, Wo):
        import jax, jax.numpy as jnp
        import numpy as np
        import math
        D_MODEL = 256
        LAYER_ID = 6
        NUM_LAYERS = 12
        B = 8
        T = 512

        def _wkv(w, u, k, v):
            wn = -jnp.exp(w)

            def step(carry, kv):
                aa, bb, pp = carry
                kt, vt = kv
                ww = u + kt
                p = jnp.maximum(pp, ww)
                e1 = jnp.exp(pp - p)
                e2 = jnp.exp(ww - p)
                y = (e1 * aa + e2 * vt) / (e1 * bb + e2)
                ww2 = pp + wn
                p2 = jnp.maximum(ww2, kt)
                e1b = jnp.exp(ww2 - p2)
                e2b = jnp.exp(kt - p2)
                return ((e1b * aa + e2b * vt, e1b * bb + e2b, p2), y)
            Bd, Td, Cd = k.shape
            init = (jnp.zeros((Bd, Cd), k.dtype), jnp.zeros((Bd, Cd), k.dtype), jnp.full((Bd, Cd), -1e+38, k.dtype))
            kT = jnp.swapaxes(k, 0, 1)
            vT = jnp.swapaxes(v, 0, 1)
            _, ys = jax.lax.scan(step, init, (kT, vT))
            return jnp.swapaxes(ys, 0, 1)
        xs = jnp.pad(x, ((0, 0), (1, 0), (0, 0)))[:, :-1]
        xk = x * time_mix_k + xs * (1.0 - time_mix_k)
        xv = x * time_mix_v + xs * (1.0 - time_mix_v)
        xr = x * time_mix_r + xs * (1.0 - time_mix_r)
        k = jnp.einsum('btc,dc->btd', xk, Wk)
        v = jnp.einsum('btc,dc->btd', xv, Wv)
        r = jnp.einsum('btc,dc->btd', xr, Wr)
        wkv = _wkv(w, u, k, v)
        rwkv = jax.nn.sigmoid(r) * wkv
        return jnp.einsum('btc,dc->btd', rwkv, Wo)

    def _L0_ffn_ref(x, Wg, ln_scale, ln_bias, W1, b1, W2, b2):
        import jax, jax.numpy as jnp
        import numpy as np
        B, T, D, E, H = (8, 512, 256, 8, 64)
        LN_EPS = 1e-05
        Bs, Ts, Ds = x.shape
        xt = x.reshape(Bs * Ts, Ds)
        logits = xt @ Wg.T
        top1 = jnp.argmax(logits, axis=-1)
        mu = jnp.mean(xt, axis=-1, keepdims=True)
        var = jnp.mean(jnp.square(xt - mu), axis=-1, keepdims=True)
        xhat = (xt - mu) * jax.lax.rsqrt(var + LN_EPS)
        n_experts = Wg.shape[0]

        def body(y, p):
            s_e, b_e, w1, bb1, w2, bb2, eid = p
            h = jax.nn.gelu((xhat * s_e + b_e) @ w1 + bb1, approximate=False)
            out = h @ w2 + bb2
            mask = (top1 == eid)[:, None].astype(out.dtype)
            return (y + mask * out, None)
        y0 = jnp.zeros_like(xt)
        y, _ = jax.lax.scan(body, y0, (ln_scale, ln_bias, W1, b1, W2, b2, jnp.arange(n_experts)))
        return y.reshape(Bs, Ts, Ds)
    h = _L0_tok_ref(x, L0_tok_scharr)
    h = h + _L0_attn_ref(_layernorm(h, axis=-1), L0_attn_w, L0_attn_u, L0_attn_time_mix_k, L0_attn_time_mix_v, L0_attn_time_mix_r, L0_attn_Wk, L0_attn_Wv, L0_attn_Wr, L0_attn_Wo)
    h = h + _L0_ffn_ref(_layernorm(h, axis=-1), L0_ffn_Wg, L0_ffn_ln_scale, L0_ffn_ln_bias, L0_ffn_W1, L0_ffn_b1, L0_ffn_W2, L0_ffn_b2)
    return h

_drawn_inputs = setup_inputs


def setup_inputs(seed=0):
    import zlib

    import numpy as np

    out = dict(_drawn_inputs(seed))
    spreads = {'L0_ffn_ln_scale': (1.0, 0.6),
     'L0_ffn_ln_bias': (0.0, 0.8),
     'L0_ffn_b1': (0.0, 0.8),
     'L0_ffn_b2': (0.0, 0.1)}
    factors = {'L0_attn_u': 4.667,
     'L0_attn_time_mix_k': 2.931,
     'L0_attn_time_mix_r': 4.915,
     'L0_ffn_W1': 5.471,
     'L0_ffn_W2': 5.185}
    for name, (base, spread) in spreads.items():
        noise = np.random.default_rng([zlib.crc32(name.encode()), seed]).standard_normal(out[name].shape)
        drawn = base * np.exp(spread * noise) if base else spread * noise
        out[name] = jnp.asarray(drawn.astype(out[name].dtype))
    for name, factor in factors.items():
        out[name] = (out[name] * factor).astype(out[name].dtype)
    return out
```

```python
import concourse.bass as bass
from concourse import mybir
from contextlib import ExitStack

F32 = mybir.dt.float32
F32R = mybir.dt.float32r
BF16 = mybir.dt.bfloat16
ALU = mybir.AluOpType
ACT = mybir.ActivationFunctionType
AXIS_X = mybir.AxisListType.X

GRAY_WEIGHTS = (0.2989, 0.587, 0.114)
LN_EPS = 1e-5
NEVER = -1e38
BONUS_CAP = 40.0
MASK_OUT = -float(2 ** 40)
GRAY, EDGE, WKV, FFN, OUT = range(5)
UNROLL = 4


class Step:

    def __init__(self, j, u, pairs):
        self.j, self.u, self.pairs = j, u, pairs

    def has(self, stage):
        return not isinstance(self.j, int) or 0 <= UNROLL * self.j + self.u - stage < self.pairs

    def buf(self, stage, n=2):
        return (self.u - stage) % n

    def count(self, stage, per_pair, k, back=0):
        v = self.j * (UNROLL * per_pair) + (per_pair * (self.u - stage - back) + k)
        return min(max(0, v), per_pair * self.pairs) if isinstance(v, int) else v

    def dma_count(self, stage, dmas, back=0):
        v = self.j * (UNROLL // 2 * 16 * dmas) + 16 * dmas * ((self.u - stage - back) // 2 + 1)
        return max(0, v) if isinstance(v, int) else v


def vision_layer(nc, x, scharr, w, u, time_mix_k, time_mix_v, time_mix_r, Wk, Wv, Wr, Wo,
                 Wg, ln_scale, ln_bias, W1, b1, W2, b2, out):
    B, NCOL, T, D = x.shape
    E, _, H = W1.shape
    P = 128
    PAIRS = B // 2
    HALF = T // P
    CH = D // P
    NB = HALF * 2
    NM = E * H // P
    assert T == 256 and D == 256 and NCOL == 3 and E == 8 and E * H == 512
    assert PAIRS % UNROLL == 0 and PAIRS // UNROLL >= 2

    ROW_W, ROW_U, ROW_TM = 0, 2, (4, 6, 8)
    ROW_SCALE, ROW_BIAS, ROW_B1 = 10, 10 + E * CH, 10 + 2 * E * CH
    ROWS = ROW_B1 + NM

    x_planes = x.rearrange("n c h w -> (n c) h w")
    gray_halo_dram = nc.dram_tensor("gray_halo_dram", [2, P, D + 2], F32).ap()

    with ExitStack() as ctx:
        def sb(name, shape, dt=F32):
            return ctx.enter_context(nc.sbuf_tensor(name, shape, dt))

        def sem(name):
            return ctx.enter_context(nc.semaphore(name))

        planes = [sb(f"planes{i}", [P, NB, NCOL, D]) for i in range(2)]
        gray = sb("gray", [P, NB, D])
        gray_hi = [sb(f"gray_hi{i}", [P, NB, D + 2], F32R) for i in range(2)]
        gray_lo = [sb(f"gray_lo{i}", [P, NB, D + 2], F32R) for i in range(2)]
        halo = [sb(f"halo{i}", [P, 2, 2, D], F32R) for i in range(2)]
        abs_a = sb("abs_a", [P, HALF, 2 * D])
        edge = [sb(f"edge{i}", [P, NB, D]) for i in range(4)]
        normed = sb("normed", [P, NB, D])
        normed_t = sb("normed_t", [P, NB, T + 1])
        step_diff = sb("step_diff", [P, NB, T])
        mixed = [sb(f"mixed_{n}", [P, NB, T]) for n in "kvr"]
        k_pad = sb("k_pad", [P, NB, T + 1])
        v_sb = sb("v_sb", [P, NB, T])
        gate = sb("gate", [P, NB, T])
        max_num = sb("max_num", [P, NB, T + 1])
        den_state = sb("den_state", [P, NB, T + 1])
        fresh = sb("fresh", [P, NB, T + 1])
        decay = sb("decay", [P, NB, T + 1])
        fresh_v = sb("fresh_v", [P, NB, T + 1])
        bonus = sb("bonus", [P, NB, T])
        den = sb("den", [P, NB, T])
        rwkv = sb("rwkv", [P, NB, T])
        resid = sb("resid", [P, NB, D])
        normed2 = sb("normed2", [P, NB, D])
        normed2_t = sb("normed2_t", [P, CH, 2, T])
        route = sb("route", [P, NB, P], BF16)
        route_t = sb("route_t", [P, 2, T], BF16)
        hidden = sb("hidden", [P, NM, 2, T])
        result = [sb(f"result{i}", [P, NB, D]) for i in range(2)]
        stats = [sb(f"stats{i}", [P, NB, 6]) for i in range(2)]
        moments = [sb(f"moments{i}", [P, NB, 2]) for i in range(2)]
        log_var = [sb(f"log_var{i}", [P, NB]) for i in range(2)]
        rstd = [sb(f"rstd{i}", [P, NB]) for i in range(2)]
        best = sb("best", [P, NB])
        rank = sb("rank", [P, NB, E])
        best_rank = sb("best_rank", [P, NB])

        ident = sb("ident", [P, P])
        ident_bf = sb("ident_bf", [P, P], BF16)
        band_hi = sb("band_hi", [P, 6, P], F32R)
        band_lo = sb("band_lo", [P, 6, P], F32R)
        band_halo = sb("band_halo", [P, 2 * HALF, P], F32R)
        params = sb("params", [P, ROWS])
        w_t = [sb(f"w_t_{n}", [P, CH, D]) for n in "kvro"]
        wg_t = sb("wg_t", [P, CH, E])
        w1_scaled = sb("w1_scaled", [P, CH, E * H])
        b1_full = sb("b1_full", [P, NM])
        w2_sb = sb("w2_sb", [P, NM, D])
        b2_parts = sb("b2_parts", [P, D], BF16)
        mask_rows = sb("mask_rows", [P, E * H], BF16)
        exp_w = sb("exp_w", [P, CH])
        decay_step = sb("decay_step", [P, NB, T + 1])
        eps = sb("eps", [P, 2])
        descending = sb("descending", [P, E])
        scharr_all = sb("scharr_all", [P, 18])
        scharr_dj = sb("scharr_dj", [P, 6])
        scharr_hi = sb("scharr_hi", [P, 6], F32R)
        scharr_lo = sb("scharr_lo", [P, 6], F32R)

        w_raw = [mixed[i // 2][:, 2 * (i % 2):2 * (i % 2) + 2, :] for i in range(4)]
        wg_raw = mixed[2][0:E, 0, :]
        params_raw = mixed[2][0:ROWS, 1, 0:P]
        b2_raw = mixed[2][:, 2, :]
        b2_rest = mixed[2][:, 3, :]
        b2_mid = rwkv[:, 0, 0:128].bitcast(BF16)
        b2_low = rwkv[:, 0, 128:256].bitcast(BF16)
        w1_raw = hidden[:, 0:2, :, :].rearrange("p a b c -> p a (b c)")
        halo_planes = v_sb[:, 0:3, :]
        halo_gray = v_sb[:, 3, :]
        halo_hi = sb("halo_hi", [P, D + 2], F32R)
        halo_lo = sb("halo_lo", [P, D + 2], F32R)
        shift = normed2[:, 0:3, 0:P]
        band = normed[:, 0:3, :].rearrange("p a (b m) -> p (a b) m", b=2)

        bank = [ctx.enter_context(nc.psum_tensor(f"bank{i}", [P, 512], F32)) for i in range(8)]
        logits = bank[7][:, 0:NB * E].rearrange("p (b e) -> p b e", b=NB)
        route_ps = bank[7][:, 256:512].bitcast(BF16)
        BANK_EDGE, BANK_WO, BANK_K, BANK_V = (0, 1, 2, 3), (4, 5), (6, 0), (1, 2)
        BANK_NORMED2, BANK_R, BANK_NORMED, BANK_HIDDEN, BANK_Y = (3, 4), (5, 6), (0, 1), (2, 3, 4, 5), (6, 7)

        planes_in = [sem(f"planes_in{i}") for i in range(2)]
        s_params_in, s_scharr_in, s_scharr_dj_in = sem("params_in"), sem("scharr_in"), sem("scharr_dj_in")
        s_w_in, s_wg_in, s_w1_in, s_w2_in = sem("w_in"), sem("wg_in"), sem("w1_in"), sem("w2_in")
        s_b2_in, s_halo_planes_in = sem("b2_in"), sem("halo_planes_in")
        s_cleared, s_built = sem("cleared"), sem("built")
        s_dve_setup, s_act_setup, s_pe_setup = sem("dve_setup"), sem("act_setup"), sem("pe_setup")

        halo_in = [sem(f"halo_in{i}") for i in range(2)]
        stored = [sem(f"stored{i}") for i in range(2)]
        s_red, s_red_green, s_gray, s_gray_hi, s_gray_lo = [sem(n) for n in (
            "red", "red_green", "gray_done", "gray_hi_done", "gray_lo_done")]
        s_edge_ps, s_abs, s_edge = sem("edge_ps"), sem("abs"), sem("edge_done")
        s_stats, s_moments, s_log_var, s_rstd = [[sem(f"{n}{i}") for i in range(2)] for n in (
            "stats", "moments", "log_var", "rstd")]
        s_normed, s_normed_ps, s_normed_t = sem("normed"), sem("normed_ps"), sem("normed_t")
        s_diff, s_mixed, s_proj_ps = sem("diff"), sem("mixed"), sem("proj_ps")
        s_k, s_v, s_gate = sem("k"), sem("v"), sem("gate")
        s_max, s_gap, s_exponents, s_exps = sem("max"), sem("gap"), sem("exponents"), sem("exps")
        s_den_state, s_den, s_fresh_v, s_num_state = [sem(n) for n in (
            "den_state", "den_done", "fresh_v_done", "num_state")]
        s_log_den, s_recip, s_bonus_v, s_num, s_gated, s_rwkv = [sem(n) for n in (
            "log_den", "recip", "bonus_v", "num", "gated", "rwkv_done")]
        s_wo_ps, s_resid = sem("wo_ps"), sem("resid_done")
        s_normed2, s_normed2_ps, s_normed2_t = sem("normed2"), sem("normed2_ps"), sem("normed2_t")
        s_logits, s_best, s_hits, s_ranked, s_best_rank, s_route, s_route_ps, s_route_t = [sem(n) for n in (
            "logits", "best_done", "hits", "ranked", "best_rank_done", "route", "route_ps", "route_t")]
        s_hidden_ps, s_hidden, s_y_ps, s_result = [sem(n) for n in (
            "hidden_ps", "hidden_done", "y_ps", "result_done")]

        def run_steps(eng, step):
            for i in range(UNROLL):
                step(Step(0, i, PAIRS))
            with eng.Fori(1, PAIRS // UNROLL) as j:
                for i in range(UNROLL):
                    step(Step(j, i, PAIRS))
            for i in range(UNROLL):
                step(Step(PAIRS // UNROLL, i, PAIRS))

        block = ctx.enter_context(nc.Block())

        @block.sync
        def _(sp):
            def load_planes(j, c, buf):
                for half in range(HALF):
                    first = j * (UNROLL * 6) + 6 * c
                    src = x_planes[bass.ds(first, 6), half * P:(half + 1) * P, :]
                    sp.dma_start(planes[buf][:, 2 * half:2 * half + 2, :, :].rearrange("p i c w -> p (i c) w"),
                                 src.rearrange("n p w -> p n w")).then_inc(planes_in[buf], 16)

            sp.dma_start(scharr_all[:, :], scharr.rearrange("o i h w -> (o i h w)")
                         .partition_broadcast(P)).then_inc(s_scharr_in, 16)
            rows = [(ROW_W, w.rearrange("(r c) -> r c", c=P)), (ROW_U, u.rearrange("(r c) -> r c", c=P))]
            rows += [(r, t.rearrange("a b (r c) -> (a b r) c", c=P))
                     for r, t in zip(ROW_TM, (time_mix_k, time_mix_v, time_mix_r))]
            rows += [(ROW_SCALE, ln_scale.rearrange("e (r c) -> (e r) c", c=P)),
                     (ROW_BIAS, ln_bias.rearrange("e (r c) -> (e r) c", c=P)),
                     (ROW_B1, b1.rearrange("e h -> (e h)").rearrange("(r c) -> r c", c=P))]
            for r, src in rows:
                sp.dma_start(params_raw[r:r + src.shape[0], :], src).then_inc(s_params_in, 16)
            for i in range(3):
                sp.dma_start(halo_planes[:, i, :], x[:, i, P - 1:P + 1, :].rearrange("n r w -> n r w")
                             ).then_inc(s_halo_planes_in, 16)
            for i in range(3):
                sp.dma_start(scharr_dj[32 * i:32 * i + 3, :], scharr.rearrange("o i h w -> w (o i h)"),
                             allow_slow_non_contiguous=True).then_inc(s_scharr_dj_in, 16)
            for src, dst in zip((Wk, Wv, Wr, Wo), w_raw):
                sp.dma_start(dst, src.rearrange("(a p) c -> p a c", p=P)).then_inc(s_w_in, 16)
            sp.dma_start(w1_raw[:, 0, :].rearrange("p (e h) -> p e h", e=E),
                         W1[:, 0:P, :].rearrange("e p h -> p e h")).then_inc(s_w1_in, 16)
            sp.dma_start(w1_raw[:, 1, :].rearrange("p (e h) -> p e h", e=E),
                         W1[:, P:2 * P, :].rearrange("e p h -> p e h")).then_inc(s_w1_in, 16)
            sp.dma_start(wg_raw, Wg).then_inc(s_wg_in, 16)
            sp.wait_ge(s_cleared, 1)
            for i in range(3):
                sp.dma_start(b2_raw[32 * i:32 * i + E, :], b2).then_inc(s_b2_in, 16)
            sp.dma_start(w2_sb[:, :, :], W2.rearrange("e h d -> (e h) d").rearrange("(m p) d -> p m d", p=P)
                         ).then_inc(s_w2_in, 16)
            sp.wait_ge(s_cleared, 2)
            sp.wait_ge(s_dve_setup, 4)
            sp.dma_start(gray_halo_dram[0], halo_hi[:, :].bitcast(F32)).then_inc(stored[0], 16)
            sp.dma_start(gray_halo_dram[1], halo_lo[:, :].bitcast(F32)).then_inc(stored[1], 16)
            for i in range(2):
                sp.wait_ge(stored[i], 16)
            sp.wait_ge(s_built, 1)

            def step(at):
                if at.has(GRAY):
                    b = at.buf(GRAY)
                    sp.wait_ge(s_gray, at.count(GRAY, 1, 1, back=2))
                    load_planes(at.j, at.u, b)
                    sp.wait_ge(s_edge_ps, at.count(GRAY, 4, 4, back=2))
                    for i, part in enumerate((0, 0, 1)):
                        row = at.j * (UNROLL * 4) + 4 * at.u
                        src = bass.AP(gray_halo_dram.tensor, part * P * (D + 2) + row * (D + 2),
                                      [[1, 3], [D + 2, 4], [1, D]])
                        dst = halo[b][32 * i:32 * i + 3, :, :, :].bitcast(F32).rearrange("p i r w -> p (i r) w")
                        sp.dma_start(dst, src).then_inc(halo_in[b], 16)
                if at.has(OUT):
                    for half in range(HALF):
                        sp.wait_ge(s_result, at.count(OUT, 2, half + 1))
                        first = at.j * (UNROLL * 2) + 2 * (at.u - OUT)
                        dst = out[bass.ds(first, 2), half * P:(half + 1) * P, :].rearrange("n p w -> p n w")
                        sp.dma_start(dst, result[at.buf(OUT)][:, 2 * half:2 * half + 2, :]
                                     ).then_inc(stored[at.buf(OUT)], 16)

            run_steps(sp, step)
            for i in range(2):
                sp.wait_ge(stored[i], 16 + 16 * HALF * PAIRS // 2)

        @block.gpsimd
        def _(pool):
            pool.memset(b2_raw, 0.0).then_inc(s_cleared, 1)
            for t in (halo_hi, halo_lo):
                pool.memset(t[:, 0:1].bitcast(F32), 0.0)
                pool.memset(t[:, D + 1:D + 2].bitcast(F32), 0.0)
            pool.memset(shift, 0.0).then_inc(s_cleared, 1)
            pool.wait_ge(s_cleared, 2)
            for di in range(3):
                pool.affine_select(out=shift[:, di, :], in_=shift[:, di, :], compare_op=ALU.not_equal, fill=1.0,
                                   base=1 - di, pattern=[[-1, P]], channel_multiplier=1).then_inc(s_cleared, 1)
            pool.memset(mask_rows[:, :], MASK_OUT).then_inc(s_cleared, 1)
            pool.wait_ge(s_cleared, 6)
            pool.affine_select(out=mask_rows[:, :], in_=mask_rows[:, :], compare_op=ALU.is_ge, fill=0.0,
                               base=96 * H, pattern=[[1, E * H]], channel_multiplier=-H).then_inc(s_cleared, 1)
            pool.wait_ge(s_cleared, 7)
            pool.affine_select(out=mask_rows[:, :], in_=mask_rows[:, :], compare_op=ALU.is_ge, fill=0.0,
                               base=H - 1 - 96 * H, pattern=[[-1, E * H]], channel_multiplier=H).then_inc(s_cleared, 1)
            for i in range(2):
                pool.memset(halo[i][:, :, :, :].bitcast(F32), 0.0)
                for g in (gray_hi[i], gray_lo[i]):
                    pool.memset(g[:, :, 0:1].bitcast(F32), 0.0)
                    pool.memset(g[:, :, D + 1:D + 2].bitcast(F32), 0.0)
            pool.memset(normed_t[:, :, 0:1], 0.0)
            pool.memset(k_pad[:, :, 0:1], NEVER)
            for t in (fresh, decay, fresh_v):
                pool.memset(t[:, :, 0:1], 0.0)
            for e in range(E):
                pool.memset(descending[:, e:e + 1], float(E - e))
            pool.memset(eps[:, 0:1], LN_EPS)
            pool.memset(eps[:, 1:2], LN_EPS * LN_EPS)
            pool.memset(band_halo[:, :, :].bitcast(F32), 0.0)
            pool.memset(b2_parts[:, :], 0.0)
            pool.memset(route[:, :, :], 0.0).then_inc(s_built, 1)

        @block.vector
        def _(dve):
            own = [0]

            def done(ins):
                own[0] += 1
                ins.then_inc(s_dve_setup, 1)
                dve.wait_ge(s_dve_setup, own[0])

            dve.wait_ge(s_halo_planes_in, 48)
            done(dve.tensor_scalar(halo_gray, halo_planes[:, 0, :], GRAY_WEIGHTS[0], None, ALU.mult))
            for i in (1, 2):
                done(dve.scalar_tensor_tensor(out=halo_gray, in0=halo_planes[:, i, :], scalar=GRAY_WEIGHTS[i],
                                              in1=halo_gray, op0=ALU.mult, op1=ALU.add))
            dve.wait_ge(s_act_setup, 1)
            done(dve.tensor_tensor(halo_lo[:, 1:D + 1], halo_gray, halo_hi[:, 1:D + 1].bitcast(F32), ALU.subtract))

            dve.wait_ge(s_scharr_in, 16)
            dve.wait_ge(s_scharr_dj_in, 48)
            dve.wait_ge(s_cleared, 5)
            done(dve.tensor_scalar(scharr_all[:, :], scharr_all[:, :], 0.5, None, ALU.mult))
            for i in range(3):
                rows = slice(32 * i, 32 * i + 3)
                dve.tensor_scalar(scharr_dj[rows, :], scharr_dj[rows, :], 0.5, None, ALU.mult)
            done(dve.tensor_copy(ident[:, :], shift[:, 1, :]))
            for i in range(3):
                rows = slice(32 * i, 32 * i + 3)
                dve.tensor_copy(scharr_hi[rows, :], scharr_dj[rows, :])
            done(dve.tensor_copy(ident_bf[:, :], ident[:, :]))
            for i in range(3):
                rows = slice(32 * i, 32 * i + 3)
                dve.tensor_tensor(scharr_lo[rows, :], scharr_dj[rows, :], scharr_hi[rows, :].bitcast(F32),
                                  ALU.subtract)
            for di in range(3):
                for c in range(2):
                    for dj in range(3):
                        weight = scharr_all[:, 9 * c + 3 * di + dj:9 * c + 3 * di + dj + 1]
                        b = band[:, 3 * c + dj, :]
                        if di == 0:
                            ins = dve.tensor_scalar(b, shift[:, di, :], weight, None, ALU.mult)
                        else:
                            ins = dve.scalar_tensor_tensor(out=b, in0=shift[:, di, :], scalar=weight, in1=b,
                                                           op0=ALU.mult, op1=ALU.add)
                done(ins)
            done(dve.tensor_copy(band_hi[:, :, :], band))
            done(dve.tensor_tensor(band_lo[:, :, :], band, band_hi[:, :, :].bitcast(F32), ALU.subtract))
            dve.wait_ge(s_built, 1)
            for half, (col, di) in enumerate(((P - 1, 2), (0, 0))):
                for c in range(2):
                    for i, part in enumerate((scharr_hi, scharr_lo, scharr_hi)):
                        rows = slice(32 * i, 32 * i + 3)
                        dve.tensor_copy(band_halo[rows, 2 * half + c, col:col + 1],
                                        part[rows, 3 * c + di:3 * c + di + 1].bitcast(F32))
            dve.wait_ge(s_pe_setup, 1)
            done(dve.tensor_copy(params[:, :], bank[0][:, 0:ROWS]))
            dve.memset(decay_step[:, :, 1:T + 1], -1.0)
            done(dve.memset(decay_step[:, :, 0:1], NEVER))
            dve.wait_ge(s_act_setup, 2)
            for ct in range(CH):
                seg = decay_step[:, 2 * ct:2 * ct + 2, 1:T + 1]
                done(dve.tensor_scalar(seg, seg, exp_w[:, ct:ct + 1], None, ALU.mult))
            dve.wait_ge(s_w1_in, 32)
            for ct in range(CH):
                cols = params[:, ROW_SCALE + ct:ROW_BIAS:CH]
                done(dve.tensor_tensor(w1_scaled[:, ct, :].rearrange("p (e h) -> p e h", e=E),
                                       w1_raw[:, ct, :].rearrange("p (e h) -> p e h", e=E),
                                       cols.unsqueeze(2).to_broadcast([P, E, H]), ALU.mult))
            dve.wait_ge(s_b2_in, 48)
            b2_high = b2_parts[:, :]
            done(dve.tensor_copy(b2_mid, b2_raw))
            done(dve.tensor_tensor(b2_rest, b2_raw, b2_mid, ALU.subtract))
            done(dve.tensor_copy(b2_high[0:E, :], b2_mid[0:E, :]))
            done(dve.tensor_copy(b2_mid, b2_rest))
            done(dve.tensor_copy(b2_high[32:32 + E, :], b2_mid[32:32 + E, :]))
            done(dve.tensor_tensor(b2_rest, b2_rest, b2_mid, ALU.subtract))
            done(dve.tensor_copy(b2_high[64:64 + E, :], b2_rest[64:64 + E, :]))
            dve.wait_ge(s_pe_setup, 3)
            for i in range(4):
                dve.tensor_copy(w_t[i][:, :, :].rearrange("p a d -> p (a d)"), bank[1 + i][:, :])
            dve.tensor_copy(wg_t[:, :, :].rearrange("p a e -> p (a e)"), bank[5][:, 0:CH * E])
            dve.wait_ge(s_pe_setup, 4)
            for m in range(NM):
                for i in range(2):
                    rows = slice(64 * i, 64 * i + 64)
                    col = m * E + 2 * m + i
                    ins = dve.tensor_tensor(b1_full[rows, m:m + 1], bank[6][rows, col:col + 1],
                                            params[rows, ROW_B1 + m:ROW_B1 + m + 1], ALU.add)
            done(ins)

            def layer_norm_moments(i, src):
                for b in range(NB):
                    ins = dve.bn_stats(stats[i][:, b, :], src[:, b, :])
                ins.then_inc(s_stats[i], 1)

            def aggregate(i):
                for b in range(NB):
                    ins = dve.bn_aggr(moments[i][:, b, :], stats[i][:, b, :])
                ins.then_inc(s_moments[i], 1)

            def residual(half, at):
                dve.wait_ge(s_result, at.count(OUT, 2, half + 1))
                dve.wait_ge(s_wo_ps, at.count(FFN, 2, half + 1))
                dve.tensor_tensor(resid[:, 2 * half:2 * half + 2, :], pair_view(bank[BANK_WO[half]]),
                                  edge[at.buf(FFN, 4)][:, 2 * half:2 * half + 2, :], ALU.add
                                  ).then_inc(s_resid, 1)

            def step(at):
                if at.has(OUT):
                    b = at.buf(OUT)
                    dve.wait_ge(stored[b], 16 + at.dma_count(OUT, 2, back=2))
                    dve.wait_ge(s_resid, at.count(OUT, 2, 2))
                    for half in range(HALF):
                        dve.wait_ge(s_y_ps, at.count(OUT, 2, half + 1))
                        dve.tensor_tensor(result[b][:, 2 * half:2 * half + 2, :], pair_view(bank[BANK_Y[half]]),
                                          resid[:, 2 * half:2 * half + 2, :], ALU.add).then_inc(s_result, 1)
                if at.has(GRAY):
                    b = at.buf(GRAY)
                    dve.wait_ge(s_red, at.count(GRAY, 1, 1))
                    dve.scalar_tensor_tensor(out=gray[:, :, :], in0=planes[b][:, :, 1, :], scalar=GRAY_WEIGHTS[1],
                                             in1=gray[:, :, :], op0=ALU.mult, op1=ALU.add).then_inc(s_red_green, 1)
                    dve.wait_ge(s_red_green, at.count(GRAY, 1, 1))
                    dve.scalar_tensor_tensor(out=gray[:, :, :], in0=planes[b][:, :, 2, :], scalar=GRAY_WEIGHTS[2],
                                             in1=gray[:, :, :], op0=ALU.mult, op1=ALU.add).then_inc(s_gray, 1)
                if at.has(EDGE):
                    h = edge[at.buf(EDGE, 4)]
                    for half in range(HALF):
                        dve.wait_ge(s_abs, at.count(EDGE, 4, 2 * half + 2))
                        hh = h[:, 2 * half:2 * half + 2, :].rearrange("p i w -> p (i w)")
                        dve.tensor_tensor(hh, hh, abs_a[:, half, :], ALU.add).then_inc(s_edge, 1)
                        if half == 0 and at.has(GRAY):
                            b = at.buf(GRAY)
                            dve.wait_ge(s_gray_hi, at.count(GRAY, 1, 1))
                            dve.wait_ge(s_edge_ps, at.count(GRAY, 4, 4, back=2))
                            dve.tensor_tensor(gray_lo[b][:, :, 1:D + 1], gray[:, :, :],
                                              gray_hi[b][:, :, 1:D + 1].bitcast(F32), ALU.subtract
                                              ).then_inc(s_gray_lo, 1)
                    dve.wait_ge(s_edge, at.count(EDGE, 2, 2))
                    layer_norm_moments(0, h)
                elif at.has(GRAY):
                    b = at.buf(GRAY)
                    dve.wait_ge(s_gray_hi, at.count(GRAY, 1, 1))
                    dve.tensor_tensor(gray_lo[b][:, :, 1:D + 1], gray[:, :, :],
                                      gray_hi[b][:, :, 1:D + 1].bitcast(F32), ALU.subtract).then_inc(s_gray_lo, 1)
                if at.has(EDGE):
                    dve.wait_ge(s_stats[0], at.count(EDGE, 1, 1))
                if at.has(FFN):
                    residual(0, at)
                if at.has(EDGE):
                    aggregate(0)
                if at.has(FFN):
                    residual(1, at)
                    dve.wait_ge(s_resid, at.count(FFN, 2, 2))
                    layer_norm_moments(1, resid)
                    dve.wait_ge(s_stats[1], at.count(FFN, 1, 1))
                if at.has(EDGE):
                    dve.wait_ge(s_rstd[0], at.count(EDGE, 1, 1))
                    dve.wait_ge(s_normed_ps, at.count(EDGE, 2, 2, back=1))
                    for b in range(NB):
                        ins = dve.tensor_scalar(normed[:, b, :], edge[at.buf(EDGE, 4)][:, b, :],
                                                moments[0][:, b, 0:1], rstd[0][:, b:b + 1],
                                                ALU.subtract, ALU.mult)
                    ins.then_inc(s_normed, 1)
                if at.has(FFN):
                    aggregate(1)
                if at.has(FFN):
                    dve.wait_ge(s_rstd[1], at.count(FFN, 1, 1))
                    dve.wait_ge(s_normed2_ps, at.count(FFN, 2, 2, back=1))
                    for b in range(NB):
                        ins = dve.tensor_scalar(normed2[:, b, :], resid[:, b, :], moments[1][:, b, 0:1],
                                                rstd[1][:, b:b + 1], ALU.subtract, ALU.mult)
                    ins.then_inc(s_normed2, 1)
                if at.has(WKV):
                    dve.wait_ge(s_k, at.count(WKV, 2, 2))
                    dve.tensor_tensor_scan(flat(max_num), flat(decay_step), flat(k_pad), 0.0,
                                           ALU.add, ALU.max).then_inc(s_max, 1)
                    dve.wait_ge(s_max, at.count(WKV, 1, 1))
                    dve.tensor_tensor(k_pad[:, :, 1:T + 1], k_pad[:, :, 1:T + 1], max_num[:, :, 0:T],
                                      ALU.subtract).then_inc(s_gap, 1)
                    dve.wait_ge(s_gap, at.count(WKV, 1, 1))
                    gap = k_pad[:, :, 1:T + 1]
                    for ct in range(CH):
                        seg = slice(2 * ct, 2 * ct + 2)
                        ins = dve.tensor_scalar(fresh[:, seg, 1:T + 1], gap[:, seg, :], exp_w[:, ct:ct + 1], 0.0,
                                                ALU.add, ALU.min)
                    ins.then_inc(s_exponents, 1)
                    for ct in range(CH):
                        seg = slice(2 * ct, 2 * ct + 2)
                        ins = dve.tensor_scalar(decay[:, seg, 1:T + 1], gap[:, seg, :], exp_w[:, ct:ct + 1], 0.0,
                                                ALU.add, ALU.max)
                    ins.then_inc(s_exponents, 1)
                    for ct in range(CH):
                        seg = slice(2 * ct, 2 * ct + 2)
                        ins = dve.tensor_scalar(bonus[:, seg, :], gap[:, seg, :],
                                                params[:, ROW_U + ct:ROW_U + ct + 1], BONUS_CAP,
                                                ALU.add, ALU.min)
                    ins.then_inc(s_exponents, 1)
                if at.has(FFN):
                    dve.wait_ge(s_logits, at.count(FFN, 1, 1))
                    dve.tensor_reduce(best[:, :], logits, AXIS_X, ALU.max).then_inc(s_best, 1)
                    dve.wait_ge(s_best, at.count(FFN, 1, 1))
                    dve.tensor_tensor(rank[:, :, :], logits, best[:, :].unsqueeze(2).to_broadcast([P, NB, E]),
                                      ALU.is_equal).then_inc(s_hits, 1)
                    dve.wait_ge(s_hits, at.count(FFN, 1, 1))
                    dve.tensor_tensor(rank[:, :, :], rank[:, :, :],
                                      descending[:, :].unsqueeze(1).to_broadcast([P, NB, E]), ALU.mult
                                      ).then_inc(s_ranked, 1)
                    dve.wait_ge(s_ranked, at.count(FFN, 1, 1))
                    dve.tensor_reduce(best_rank[:, :], rank[:, :, :], AXIS_X, ALU.max).then_inc(s_best_rank, 1)
                    dve.wait_ge(s_best_rank, at.count(FFN, 1, 1))
                    dve.wait_ge(s_route_ps, at.count(FFN, 1, 1, back=1))
                    for i in range(4):
                        ins = dve.tensor_tensor(route[:, :, 32 * i:32 * i + E], rank[:, :, :],
                                                best_rank[:, :].unsqueeze(2).to_broadcast([P, NB, E]),
                                                ALU.is_equal if i < 3 else ALU.not_equal)
                    ins.then_inc(s_route, 1)
                if at.has(WKV):
                    dve.wait_ge(s_exps, at.count(WKV, 3, 2))
                    dve.tensor_tensor_scan(flat(den_state), flat(decay), flat(fresh), 0.0,
                                           ALU.mult, ALU.add).then_inc(s_den_state, 1)
                    dve.wait_ge(s_v, at.count(WKV, 2, 2))
                    dve.tensor_tensor(fresh_v[:, :, 1:T + 1], fresh[:, :, 1:T + 1], v_sb[:, :, :],
                                      ALU.mult).then_inc(s_fresh_v, 1)
                    dve.wait_ge(s_exps, at.count(WKV, 3, 3))
                    dve.wait_ge(s_den_state, at.count(WKV, 1, 1))
                    dve.tensor_tensor(den[:, :, :], bonus[:, :, :], den_state[:, :, 0:T],
                                      ALU.add).then_inc(s_den, 1)
                    dve.tensor_tensor(bonus[:, :, :], bonus[:, :, :], v_sb[:, :, :], ALU.mult
                                      ).then_inc(s_bonus_v, 1)
                    dve.wait_ge(s_fresh_v, at.count(WKV, 1, 1))
                    dve.tensor_tensor_scan(flat(max_num), flat(decay), flat(fresh_v), 0.0,
                                           ALU.mult, ALU.add).then_inc(s_num_state, 1)
                    dve.wait_ge(s_num_state, at.count(WKV, 1, 1))
                    dve.wait_ge(s_bonus_v, at.count(WKV, 1, 1))
                    dve.tensor_tensor(bonus[:, :, :], bonus[:, :, :], max_num[:, :, 0:T], ALU.add
                                      ).then_inc(s_num, 1)
                    dve.wait_ge(s_num, at.count(WKV, 1, 1))
                    dve.wait_ge(s_gate, at.count(WKV, 2, 2))
                    dve.tensor_tensor(bonus[:, :, :], bonus[:, :, :], gate[:, :, :], ALU.mult
                                      ).then_inc(s_gated, 1)
                if at.has(EDGE):
                    dve.wait_ge(s_normed_t, at.count(EDGE, 2, 2))
                    dve.tensor_tensor(step_diff[:, :, :], normed_t[:, :, 1:T + 1], normed_t[:, :, 0:T],
                                      ALU.subtract).then_inc(s_diff, 1)
                if at.has(WKV):
                    dve.wait_ge(s_gated, at.count(WKV, 1, 1))
                    dve.wait_ge(s_recip, at.count(WKV, 1, 1))
                    dve.wait_ge(s_wo_ps, at.count(WKV, 2, 2, back=1))
                    dve.tensor_tensor(rwkv[:, :, :], bonus[:, :, :], den[:, :, :], ALU.mult).then_inc(s_rwkv, 1)
                if at.has(EDGE):
                    dve.wait_ge(s_diff, at.count(EDGE, 1, 1))
                    for i in range(3):
                        dve.wait_ge(s_proj_ps, at.count(EDGE, 6, 2 * i + 2, back=1))
                        for ct in range(CH):
                            seg = slice(2 * ct, 2 * ct + 2)
                            ins = dve.scalar_tensor_tensor(
                                out=mixed[i][:, seg, :], in0=step_diff[:, seg, :],
                                scalar=params[:, ROW_TM[i] + ct:ROW_TM[i] + ct + 1],
                                in1=normed_t[:, seg, 0:T], op0=ALU.mult, op1=ALU.add)
                        ins.then_inc(s_mixed, 1)

            def flat(t):
                return t[:, :, :].rearrange("p s t -> p (s t)")

            def pair_view(ps):
                return ps[:, :].rearrange("p (i w) -> p i w", i=2)

            run_steps(dve, step)

        @block.scalar
        def _(act):
            act.wait_ge(s_dve_setup, 3)
            act.activation(halo_hi[:, 1:D + 1], halo_gray, ACT.Copy).then_inc(s_act_setup, 1)
            act.wait_ge(s_dve_setup, 13)
            act.activation(exp_w[:, :], params[:, ROW_W:ROW_W + CH], ACT.Exp).then_inc(s_act_setup, 1)

            def reciprocal_std(i, stage, at):
                act.preload_act_table_set("natural_log_exp_and_others")
                act.wait_ge(s_moments[i], at.count(stage, 1, 1))
                act.activation(log_var[i][:, :], moments[i][:, :, 1], ACT.Ln, bias=eps[:, i:i + 1],
                               scale=1.0 if i == 0 else 1.0 + LN_EPS).then_inc(s_log_var[i], 1)
                act.wait_ge(s_log_var[i], at.count(stage, 1, 1))
                act.activation(rstd[i][:, :], log_var[i][:, :], ACT.Exp, scale=-0.5).then_inc(s_rstd[i], 1)

            def absolute(half, at):
                act.wait_ge(s_edge, at.count(EDGE, 2, half + 1, back=1))
                act.wait_ge(s_resid, at.count(EDGE, 2, 2, back=3))
                for c, dst in enumerate((abs_a[:, half, :], edge[at.buf(EDGE, 4)][:, 2 * half:2 * half + 2, :]
                                         .rearrange("p i w -> p (i w)"))):
                    act.wait_ge(s_edge_ps, at.count(EDGE, 4, 2 * half + c + 1))
                    act.activation(dst, bank[BANK_EDGE[2 * half + c]][:, :], ACT.Abs).then_inc(s_abs, 1)

            def step(at):
                if at.has(GRAY):
                    b = at.buf(GRAY)
                    act.wait_ge(planes_in[b], at.dma_count(GRAY, 2))
                    act.wait_ge(s_gray_lo, at.count(GRAY, 1, 1, back=1))
                    act.activation(gray[:, :, :], planes[b][:, :, 0, :], ACT.Copy, scale=GRAY_WEIGHTS[0]
                                   ).then_inc(s_red, 1)
                if at.has(EDGE):
                    absolute(0, at)
                if at.has(GRAY):
                    b = at.buf(GRAY)
                    act.wait_ge(s_gray, at.count(GRAY, 1, 1))
                    act.wait_ge(s_edge_ps, at.count(GRAY, 4, 4, back=2))
                    act.activation(gray_hi[b][:, :, 1:D + 1], gray[:, :, :], ACT.Copy).then_inc(s_gray_hi, 1)
                if at.has(EDGE):
                    absolute(1, at)
                    reciprocal_std(0, EDGE, at)
                if at.has(FFN):
                    reciprocal_std(1, FFN, at)
                if at.has(WKV):
                    act.wait_ge(s_exponents, at.count(WKV, 3, 3, back=1))
                    for ct in range(CH):
                        act.wait_ge(s_proj_ps, at.count(WKV, 6, 1 + ct))
                        act.activation(k_pad[:, 2 * ct:2 * ct + 2, 1:T + 1], pair_view(bank[BANK_K[ct]]), ACT.Copy
                                       ).then_inc(s_k, 1)
                    act.wait_ge(s_bonus_v, at.count(WKV, 1, 1, back=1))
                    for ct in range(CH):
                        act.wait_ge(s_proj_ps, at.count(WKV, 6, 3 + ct))
                        act.activation(v_sb[:, 2 * ct:2 * ct + 2, :], pair_view(bank[BANK_V[ct]]), ACT.Copy
                                       ).then_inc(s_v, 1)
                if at.has(FFN):
                    act.wait_ge(s_hidden_ps, at.count(FFN, 4, 4, back=1))
                    for ct in range(CH):
                        act.wait_ge(s_normed2_ps, at.count(FFN, 2, ct + 1))
                        act.activation(normed2_t[:, ct, :, :], pair_view(bank[BANK_NORMED2[ct]]), ACT.Copy
                                       ).then_inc(s_normed2_t, 1)
                if at.has(WKV):
                    act.preload_act_table_set("natural_log_exp_and_others")
                    for i, (t, sign) in enumerate(((fresh[:, :, 1:T + 1], 1.0), (decay[:, :, 1:T + 1], -1.0),
                                                   (bonus[:, :, :], 1.0))):
                        act.wait_ge(s_exponents, at.count(WKV, 3, i + 1))
                        act.activation(t, t, ACT.Exp, scale=sign).then_inc(s_exps, 1)
                if at.has(FFN):
                    act.wait_ge(s_route_ps, at.count(FFN, 1, 1))
                    act.wait_ge(s_y_ps, at.count(FFN, 2, 2, back=1))
                    act.activation(route_t[:, :, :].rearrange("p i t -> p (i t)"), route_ps, ACT.Copy
                                   ).then_inc(s_route_t, 1)
                if at.has(EDGE):
                    act.wait_ge(s_mixed, at.count(EDGE, 3, 3, back=1))
                    for ct in range(CH):
                        act.wait_ge(s_normed_ps, at.count(EDGE, 2, ct + 1))
                        act.activation(normed_t[:, 2 * ct:2 * ct + 2, 1:T + 1], pair_view(bank[BANK_NORMED[ct]]),
                                       ACT.Copy).then_inc(s_normed_t, 1)
                if at.has(WKV):
                    act.wait_ge(s_gated, at.count(WKV, 1, 1, back=1))
                    for ct in range(CH):
                        act.wait_ge(s_proj_ps, at.count(WKV, 6, 5 + ct))
                        act.activation(gate[:, 2 * ct:2 * ct + 2, :], pair_view(bank[BANK_R[ct]]), ACT.Sigmoid
                                       ).then_inc(s_gate, 1)
                    act.preload_act_table_set("natural_log_exp_and_others")
                    act.wait_ge(s_den, at.count(WKV, 1, 1))
                    act.activation(den[:, :, :], den[:, :, :], ACT.Ln).then_inc(s_log_den, 1)
                    act.wait_ge(s_log_den, at.count(WKV, 1, 1))
                    act.activation(den[:, :, :], den[:, :, :], ACT.Exp, scale=-1.0).then_inc(s_recip, 1)
                if at.has(FFN):
                    for m in range(NM):
                        act.wait_ge(s_hidden_ps, at.count(FFN, 4, m + 1))
                        act.activation(hidden[:, m, :, :], pair_view(bank[BANK_HIDDEN[m]]), ACT.Gelu,
                                       bias=b1_full[:, m:m + 1]).then_inc(s_hidden, 1)

            def pair_view(ps):
                return ps[:, :].rearrange("p (i w) -> p i w", i=2)

            act.wait_ge(s_dve_setup, SETUP_OPS)
            run_steps(act, step)

        @block.tensor
        def _(pe):
            pe.wait_ge(s_dve_setup, 6)
            pe.wait_ge(s_params_in, 16 * 8)
            pe.transpose(bank[0][:, 0:ROWS], params_raw, ident[0:ROWS, 0:ROWS]).then_inc(s_pe_setup, 1)
            pe.wait_ge(s_w_in, 64)
            for i in range(4):
                for ct in range(CH):
                    for dt in range(CH):
                        ins = pe.transpose(bank[1 + i][:, ct * D + dt * P:ct * D + (dt + 1) * P],
                                           w_raw[i][:, dt, ct * P:(ct + 1) * P], ident[:, :])
            ins.then_inc(s_pe_setup, 1)
            pe.wait_ge(s_wg_in, 16)
            for ct in range(CH):
                ins = pe.transpose(bank[5][:, ct * E:(ct + 1) * E], wg_raw[:, ct * P:(ct + 1) * P], ident[0:E, 0:E])
            ins.then_inc(s_pe_setup, 1)
            pe.wait_ge(s_w1_in, 32)
            pe.wait_ge(s_dve_setup, 13)
            for m in range(NM):
                for ct in range(CH):
                    ins = pe.matmul(bank[6][:, m * E:(m + 1) * E], w1_raw[:, ct, m * P:(m + 1) * P],
                                    params[:, ROW_BIAS + ct:ROW_B1:CH], start=(ct == 0), stop=(ct == CH - 1))
            ins.then_inc(s_pe_setup, 1)
            pe.wait_ge(s_w2_in, 16)
            pe.wait_ge(s_dve_setup, SETUP_OPS)
            pe.wait_ge(s_cleared, 8)

            def project(at, i, ct, dst):
                for kt in range(CH):
                    ins = pe.matmul(dst[:, :], w_t[i][:, kt, ct * P:(ct + 1) * P],
                                    mixed[i][:, 2 * kt:2 * kt + 2, :].rearrange("p i t -> p (i t)"),
                                    start=(kt == 0), stop=(kt == CH - 1))
                ins.then_inc(s_proj_ps, 1)

            def step(at):
                if at.has(EDGE):
                    b = at.buf(EDGE)
                    pe.wait_ge(s_gray_lo, at.count(EDGE, 1, 1))
                    pe.wait_ge(halo_in[b], at.dma_count(EDGE, 3))
                    for half in range(HALF):
                        for c in range(2):
                            if half == 0:
                                pe.wait_ge(s_normed_t, at.count(EDGE, 2, 1 + c, back=1))
                            else:
                                pe.wait_ge(s_hidden, at.count(OUT, 4, 1 + c))
                            ps = bank[BANK_EDGE[2 * half + c]]
                            for dj in range(3):
                                for n, (weights, part) in enumerate(((band_hi, gray_hi[b]), (band_lo, gray_hi[b]),
                                                                     (band_hi, gray_lo[b]))):
                                    pe.matmul(ps[:, :], weights[:, 3 * c + dj, :],
                                              part[:, 2 * half:2 * half + 2, dj:dj + D],
                                              start=(dj == 0 and n == 0), stop=False)
                            pe.matmul(ps[:, :], band_halo[:, 2 * half + c, :], halo[b][:, :, 1 - half, :],
                                      start=False, stop=True).then_inc(s_edge_ps, 1)
                if at.has(FFN):
                    pe.wait_ge(s_rwkv, at.count(FFN, 1, 1))
                    for half in range(HALF):
                        pe.wait_ge(s_hidden, at.count(OUT, 4, 3 + half))
                        for i in range(2):
                            for kt in range(CH):
                                ins = pe.matmul(bank[BANK_WO[half]][:, i * D:(i + 1) * D],
                                                rwkv[:, 2 * kt + i, half * P:(half + 1) * P], w_t[3][:, kt, :],
                                                start=(kt == 0), stop=(kt == CH - 1))
                        ins.then_inc(s_wo_ps, 1)
                if at.has(WKV):
                    pe.wait_ge(s_mixed, at.count(WKV, 3, 1))
                    pe.wait_ge(s_result, at.count(OUT, 2, 1))
                    project(at, 0, 0, bank[BANK_K[0]])
                    pe.wait_ge(s_abs, at.count(EDGE, 4, 1))
                    project(at, 0, 1, bank[BANK_K[1]])
                    pe.wait_ge(s_mixed, at.count(WKV, 3, 2))
                    pe.wait_ge(s_abs, at.count(EDGE, 4, 2))
                    project(at, 1, 0, bank[BANK_V[0]])
                    pe.wait_ge(s_abs, at.count(EDGE, 4, 3))
                    project(at, 1, 1, bank[BANK_V[1]])
                if at.has(FFN):
                    pe.wait_ge(s_normed2, at.count(FFN, 1, 1))
                    pe.wait_ge(s_abs, at.count(EDGE, 4, 4))
                    for ct in range(CH):
                        for i in range(2):
                            for half in range(HALF):
                                col = i * T + half * P
                                ins = pe.transpose(bank[BANK_NORMED2[ct]][:, col:col + P],
                                                   normed2[:, 2 * half + i, ct * P:(ct + 1) * P], ident[:, :])
                        ins.then_inc(s_normed2_ps, 1)
                if at.has(WKV):
                    pe.wait_ge(s_mixed, at.count(WKV, 3, 3))
                    pe.wait_ge(s_resid, at.count(FFN, 2, 2))
                    project(at, 2, 0, bank[BANK_R[0]])
                if at.has(FFN):
                    pe.wait_ge(s_normed2_t, at.count(FFN, 2, 2))
                    pe.wait_ge(s_result, at.count(OUT, 2, 2))
                    for half in range(HALF):
                        for i in range(2):
                            for kt in range(CH):
                                ins = pe.matmul(logits[:, 2 * half + i, :],
                                                normed2_t[:, kt, i, half * P:(half + 1) * P], wg_t[:, kt, :],
                                                start=(kt == 0), stop=(kt == CH - 1))
                    ins.then_inc(s_logits, 1)
                if at.has(WKV):
                    pe.wait_ge(s_k, at.count(WKV, 2, 1))
                    project(at, 2, 1, bank[BANK_R[1]])
                if at.has(EDGE):
                    pe.wait_ge(s_normed, at.count(EDGE, 1, 1))
                    for ct in range(CH):
                        if ct == 0:
                            pe.wait_ge(s_k, at.count(WKV, 2, 2))
                        else:
                            pe.wait_ge(s_v, at.count(WKV, 2, 1))
                        for i in range(2):
                            for half in range(HALF):
                                col = i * T + half * P
                                ins = pe.transpose(bank[BANK_NORMED[ct]][:, col:col + P],
                                                   normed[:, 2 * half + i, ct * P:(ct + 1) * P], ident[:, :])
                        ins.then_inc(s_normed_ps, 1)
                if at.has(FFN):
                    pe.wait_ge(s_route, at.count(FFN, 1, 1))
                    for i in range(2):
                        for half in range(HALF):
                            col = i * T + half * P
                            ins = pe.transpose(route_ps[:, col:col + P], route[:, 2 * half + i, :], ident_bf[:, :])
                    ins.then_inc(s_route_ps, 1)
                    pe.wait_ge(s_route_t, at.count(FFN, 1, 1))
                    for m in range(NM):
                        ps = bank[BANK_HIDDEN[m]]
                        if m == 0:
                            pe.wait_ge(s_v, at.count(WKV, 2, 2))
                        elif m < 3:
                            pe.wait_ge(s_normed2_t, at.count(FFN, 2, m))
                        else:
                            pe.wait_ge(s_gate, at.count(WKV, 2, 1))
                        for kt in range(CH):
                            pe.matmul(ps[:, :], w1_scaled[:, kt, m * P:(m + 1) * P],
                                      normed2_t[:, kt, :, :].rearrange("p i t -> p (i t)"),
                                      start=(kt == 0), stop=False)
                        pe.matmul(ps[:, :], mask_rows[:, m * P:(m + 1) * P],
                                  route_t[:, :, :].rearrange("p i t -> p (i t)"),
                                  start=False, stop=True).then_inc(s_hidden_ps, 1)
                    pe.wait_ge(s_hidden, at.count(FFN, 4, 4))
                    pe.wait_ge(s_gate, at.count(WKV, 2, 2))
                    for half in range(HALF):
                        for i in range(2):
                            ps = bank[BANK_Y[half]][:, i * D:(i + 1) * D]
                            rows = slice(half * P, (half + 1) * P)
                            for m in range(NM):
                                pe.matmul(ps, hidden[:, m, i, rows], w2_sb[:, m, :], start=(m == 0), stop=False)
                            ins = pe.matmul(ps, route_t[:, i, rows], b2_parts[:, :], start=False, stop=True)
                        ins.then_inc(s_y_ps, 1)

            run_steps(pe, step)


SETUP_OPS = 26


_INS = ['x', 'L0_tok_scharr', 'L0_attn_w', 'L0_attn_u', 'L0_attn_time_mix_k', 'L0_attn_time_mix_v',
        'L0_attn_time_mix_r', 'L0_attn_Wk', 'L0_attn_Wv', 'L0_attn_Wr', 'L0_attn_Wo', 'L0_ffn_Wg',
        'L0_ffn_ln_scale', 'L0_ffn_ln_bias', 'L0_ffn_W1', 'L0_ffn_b1', 'L0_ffn_W2', 'L0_ffn_b2']
_OUTS = [((64, 256, 256), 'float32')]


def kernel(**inputs):
    import numpy as _np
    import concourse.bacc as _bacc
    from concourse import mybir as _mybir
    from concourse.bass_utils import run_bass_kernel_spmd as _run

    nc = _bacc.Bacc("TRN2", target_bir_lowering=False, num_devices=1)
    arrays, args = {}, []
    for name in _INS:
        a = _np.ascontiguousarray(inputs[name])
        arrays[f"in_{name}_dram"] = a
        args.append(nc.dram_tensor(f"in_{name}_dram", a.shape, _mybir.dt.from_np(a.dtype), kind="ExternalInput").ap())
    for i, (shape, dtype) in enumerate(_OUTS):
        dt = _mybir.dt.from_np(_np.dtype(dtype))
        args.append(nc.dram_tensor(f"out_{i}_dram", shape, dt, kind="ExternalOutput").ap())
    vision_layer(nc, *args)
    r = _run(nc, [arrays], core_ids=[0])
    got = tuple(r.results[0][f"out_{i}_dram"] for i in range(len(_OUTS)))
    return got[0]
```

```python
import concourse.bass as bass
from concourse import mybir
from contextlib import ExitStack

F32 = mybir.dt.float32
F32R = mybir.dt.float32r
BF16 = mybir.dt.bfloat16
ALU = mybir.AluOpType
ACT = mybir.ActivationFunctionType
AXIS_X = mybir.AxisListType.X

GRAY_WEIGHTS = (0.2989, 0.587, 0.114)
LN_EPS = 1e-5
NEVER = -1e38
BONUS_CAP = 40.0
MASK_OUT = -float(2 ** 40)
GRAY, EDGE, WKV, PROJ, FFN = range(5)
RESULTS_AHEAD = 2
UNROLL = 4


class Step:

    def __init__(self, j, u, pairs):
        self.j, self.u, self.pairs = j, u, pairs

    def has(self, stage):
        return not isinstance(self.j, int) or 0 <= UNROLL * self.j + self.u - stage < self.pairs

    def buf(self, stage, n=2):
        return (self.u - stage) % n

    def count(self, stage, per_pair, k, back=0):
        v = self.j * (UNROLL * per_pair) + (per_pair * (self.u - stage - back) + k)
        return min(max(0, v), per_pair * self.pairs) if isinstance(v, int) else v

    def dma_count(self, stage, dmas, n=2, back=0):
        v = self.j * (UNROLL // n * 16 * dmas) + 16 * dmas * ((self.u - stage - back) // n + 1)
        return max(0, v) if isinstance(v, int) else v

    def results(self, k, back=0):
        return RESULTS_AHEAD + self.count(FFN, 2, k, back)


def vision_layer(nc, x, scharr, w, u, time_mix_k, time_mix_v, time_mix_r, Wk, Wv, Wr, Wo,
                 Wg, ln_scale, ln_bias, W1, b1, W2, b2, out):
    B, NCOL, T, D = x.shape
    E, _, H = W1.shape
    P = 128
    PAIRS = B // 2
    HALF = T // P
    CH = D // P
    NB = HALF * 2
    NM = E * H // P
    assert T == 256 and D == 256 and NCOL == 3 and E == 8 and E * H == 512
    assert PAIRS % UNROLL == 0 and PAIRS // UNROLL >= 2

    ROW_W, ROW_U, ROW_TM = 0, 2, (4, 6, 8)
    ROW_SCALE, ROW_BIAS, ROW_B1 = 10, 10 + E * CH, 10 + 2 * E * CH
    ROWS = ROW_B1 + NM

    x_planes = x.rearrange("n c h w -> (n c) h w")
    gray_halo_dram = nc.dram_tensor("gray_halo_dram", [2, P, D + 2], F32).ap()

    with ExitStack() as ctx:
        def sb(name, shape, dt=F32):
            return ctx.enter_context(nc.sbuf_tensor(name, shape, dt))

        def sem(name):
            return ctx.enter_context(nc.semaphore(name))

        planes = [sb(f"planes{i}", [P, NB, NCOL, D]) for i in range(2)]
        gray = sb("gray", [P, NB, D])
        gray_hi = sb("gray_hi", [P, NB, D + 2], F32R)
        gray_lo = sb("gray_lo", [P, NB, D + 2], F32R)
        halo = sb("halo", [P, 2, 2, D], F32R)
        abs_a = sb("abs_a", [P, HALF, 2 * D])
        edge = [sb(f"edge{i}", [P, NB, D]) for i in range(4)]
        normed = sb("normed", [P, NB, D])
        normed_t = sb("normed_t", [P, NB, T + 1])
        step_diff = normed
        mixed = [sb(f"mixed_{n}", [P, NB, T]) for n in "kvr"]
        k_pad = sb("k_pad", [P, NB, T + 1])
        v_sb = sb("v_sb", [P, NB, T])
        gate = sb("gate", [P, NB, T])
        max_num = sb("max_num", [P, NB, T + 1])
        den_state = sb("den_state", [P, NB, T + 1])
        fresh = sb("fresh", [P, NB, T + 1])
        decay = sb("decay", [P, NB, T + 1])
        fresh_v = sb("fresh_v", [P, NB, T + 1])
        bonus = sb("bonus", [P, NB, T])
        den = sb("den", [P, NB, T])
        rwkv = sb("rwkv", [P, NB, T])
        resid = [sb(f"resid{i}", [P, NB, D]) for i in range(2)]
        normed2 = sb("normed2", [P, NB, D])
        normed2_hi = sb("normed2_hi", [P, CH, 2, T], F32R)
        normed2_lo = sb("normed2_lo", [P, CH, 2, T], F32R)
        route = sb("route", [P, NB, P], BF16)
        route_t = sb("route_t", [P, 2, T], BF16)
        hidden = sb("hidden", [P, NM, 2, T])
        stats = [sb(f"stats{i}", [P, NB, 6]) for i in range(2)]
        moments = [sb(f"moments{i}", [P, NB, 2]) for i in range(2)]
        log_var = [sb(f"log_var{i}", [P, NB]) for i in range(2)]
        rstd = [sb(f"rstd{i}", [P, NB]) for i in range(2)]
        logits = sb("logits", [P, NB, E])
        best = sb("best", [P, NB])
        rank = sb("rank", [P, NB, E])
        best_rank = sb("best_rank", [P, NB])

        ident = sb("ident", [P, P])
        ident_bf = sb("ident_bf", [P, P], BF16)
        band_hi = sb("band_hi", [P, 6, P], F32R)
        band_lo = sb("band_lo", [P, 6, P], F32R)
        band_halo = sb("band_halo", [P, 2 * HALF, P], F32R)
        params = sb("params", [P, ROWS])
        w_t = [sb(f"w_t_{n}", [P, CH, D]) for n in "kvro"]
        wg_parts = sb("wg_parts", [P, CH, 2 * E], F32R)
        w1_hi, w1_lo = [sb(f"w1_{n}", [P, CH, E * H], F32R) for n in ("hi", "lo")]
        b1_full = sb("b1_full", [P, NM])
        w2_sb = sb("w2_sb", [P, NM, D])
        b2_parts = sb("b2_parts", [P, D], BF16)
        mask_rows = sb("mask_rows", [P, E * H], BF16)
        exp_w = sb("exp_w", [P, CH])
        cap_less_u = sb("cap_less_u", [P, CH])
        cap = sb("cap", [P, 1])
        decay_step = sb("decay_step", [P, NB, T + 1])
        eps = sb("eps", [P, 2])
        descending = sb("descending", [P, E])
        scharr_all = sb("scharr_all", [P, 18])
        scharr_dj = sb("scharr_dj", [P, 6])
        scharr_hi = sb("scharr_hi", [P, 6], F32R)
        scharr_lo = sb("scharr_lo", [P, 6], F32R)

        w_raw = [mixed[i // 2][:, 2 * (i % 2):2 * (i % 2) + 2, :] for i in range(4)]
        wg_raw = mixed[2][0:E, 0, :]
        params_raw = mixed[2][0:ROWS, 1, 0:P]
        b2_raw = mixed[2][:, 2, :]
        b2_rest = mixed[2][:, 3, :]
        b2_mid = rwkv[:, 0, 0:128].bitcast(BF16)
        b2_low = rwkv[:, 0, 128:256].bitcast(BF16)
        w1_raw = hidden[:, 0:2, :, :].rearrange("p a b c -> p a (b c)")
        halo_planes = v_sb[:, 0:3, :]
        halo_gray = v_sb[:, 3, :]
        halo_hi, halo_lo = [t[:, 0, :, :].rearrange("p i t -> p (i t)")[:, 0:D + 2]
                            for t in (normed2_hi, normed2_lo)]
        w1_scaled = resid[0][:, :, :].rearrange("p (a b) d -> p a (b d)", a=CH)
        shift = normed2[:, 0:3, 0:P]
        band = normed[:, 0:3, :].rearrange("p a (b m) -> p (a b) m", b=2)

        bank = [ctx.enter_context(nc.psum_tensor(f"bank{i}", [P, 512], F32)) for i in range(8)]
        logits_parts = bank[7][:, 0:NB * 2 * E].rearrange("p (b e) -> p b e", b=NB)
        route_ps = bank[2][:, 0:256].bitcast(BF16)
        BANK_EDGE, BANK_WO, BANK_K, BANK_V, BANK_R = (0, 1, 2, 3), (4, 5), (6, 7), (0, 1), (7, 0)
        BANK_HIDDEN, BANK_NORMED2, BANK_Y, BANK_NORMED = (3, 4, 5, 6), (1, 2), (3, 4), (5, 6)

        planes_in = [sem(f"planes_in{i}") for i in range(2)]
        s_params_in, s_scharr_in, s_scharr_dj_in = sem("params_in"), sem("scharr_in"), sem("scharr_dj_in")
        s_w_in, s_wg_in, s_w1_in, s_w2_in = sem("w_in"), sem("wg_in"), sem("w1_in"), sem("w2_in")
        s_b2_in, s_halo_planes_in = sem("b2_in"), sem("halo_planes_in")
        s_cleared, s_built = sem("cleared"), sem("built")
        s_dve_setup, s_act_setup, s_pe_setup = sem("dve_setup"), sem("act_setup"), sem("pe_setup")

        halo_in = sem("halo_in")
        stored = [sem(f"stored{i}") for i in range(4)]
        s_red, s_red_green, s_gray, s_gray_hi, s_gray_lo = [sem(n) for n in (
            "red", "red_green", "gray_done", "gray_hi_done", "gray_lo_done")]
        s_edge_ps, s_abs, s_edge = sem("edge_ps"), sem("abs"), sem("edge_done")
        s_stats, s_moments, s_log_var, s_rstd = [[sem(f"{n}{i}") for i in range(2)] for n in (
            "stats", "moments", "log_var", "rstd")]
        s_normed, s_normed_ps, s_normed_t = sem("normed"), sem("normed_ps"), sem("normed_t")
        s_diff, s_mixed, s_proj_ps = sem("diff"), sem("mixed"), sem("proj_ps")
        s_k, s_v, s_gate = sem("k"), sem("v"), sem("gate")
        s_max, s_gap, s_exponents, s_decay_arg, s_cap_arg, s_exps = [sem(n) for n in (
            "max", "gap", "exponents", "decay_arg", "cap_arg", "exps")]
        s_den_state, s_den, s_fresh_v, s_num_state = [sem(n) for n in (
            "den_state", "den_done", "fresh_v_done", "num_state")]
        s_log_den, s_recip, s_bonus_v, s_num, s_gated, s_rwkv = [sem(n) for n in (
            "log_den", "recip", "bonus_v", "num", "gated", "rwkv_done")]
        s_wo_ps, s_resid = sem("wo_ps"), sem("resid_done")
        s_normed2, s_normed2_ps, s_normed2_hi, s_normed2_lo = [sem(n) for n in (
            "normed2_done", "normed2_ps", "normed2_hi_done", "normed2_lo_done")]
        s_normed_i = (s_normed, s_normed2)
        s_logits_sum = sem("logits_sum")
        s_logits, s_best, s_hits, s_ranked, s_best_rank, s_route, s_route_ps, s_route_t = [sem(n) for n in (
            "logits", "best_done", "hits", "ranked", "best_rank_done", "route", "route_ps", "route_t")]
        s_hidden_ps, s_hidden, s_y_ps, s_result = [sem(n) for n in (
            "hidden_ps", "hidden_done", "y_ps", "result_done")]

        def run_steps(eng, step):
            for i in range(UNROLL):
                step(Step(0, i, PAIRS))
            with eng.Fori(1, PAIRS // UNROLL) as j:
                for i in range(UNROLL):
                    step(Step(j, i, PAIRS))
            for i in range(UNROLL):
                step(Step(PAIRS // UNROLL, i, PAIRS))

        block = ctx.enter_context(nc.Block())

        @block.sync
        def _(sp):
            def load_planes(j, c, buf):
                for half in range(HALF):
                    first = j * (UNROLL * 6) + 6 * c
                    src = x_planes[bass.ds(first, 6), half * P:(half + 1) * P, :]
                    sp.dma_start(planes[buf][:, 2 * half:2 * half + 2, :, :].rearrange("p i c w -> p (i c) w"),
                                 src.rearrange("n p w -> p n w")).then_inc(planes_in[buf], 16)

            sp.dma_start(scharr_all[:, :], scharr.rearrange("o i h w -> (o i h w)")
                         .partition_broadcast(P)).then_inc(s_scharr_in, 16)
            rows = [(ROW_W, w.rearrange("(r c) -> r c", c=P)), (ROW_U, u.rearrange("(r c) -> r c", c=P))]
            rows += [(r, t.rearrange("a b (r c) -> (a b r) c", c=P))
                     for r, t in zip(ROW_TM, (time_mix_k, time_mix_v, time_mix_r))]
            rows += [(ROW_SCALE, ln_scale.rearrange("e (r c) -> (e r) c", c=P)),
                     (ROW_BIAS, ln_bias.rearrange("e (r c) -> (e r) c", c=P)),
                     (ROW_B1, b1.rearrange("e h -> (e h)").rearrange("(r c) -> r c", c=P))]
            for r, src in rows:
                sp.dma_start(params_raw[r:r + src.shape[0], :], src).then_inc(s_params_in, 16)
            for i in range(3):
                sp.dma_start(halo_planes[:, i, :], x[:, i, P - 1:P + 1, :].rearrange("n r w -> n r w")
                             ).then_inc(s_halo_planes_in, 16)
            for i in range(3):
                sp.dma_start(scharr_dj[32 * i:32 * i + 3, :], scharr.rearrange("o i h w -> w (o i h)"),
                             allow_slow_non_contiguous=True).then_inc(s_scharr_dj_in, 16)
            for src, dst in zip((Wk, Wv, Wr, Wo), w_raw):
                sp.dma_start(dst, src.rearrange("(a p) c -> p a c", p=P)).then_inc(s_w_in, 16)
            sp.dma_start(w1_raw[:, 0, :].rearrange("p (e h) -> p e h", e=E),
                         W1[:, 0:P, :].rearrange("e p h -> p e h")).then_inc(s_w1_in, 16)
            sp.dma_start(w1_raw[:, 1, :].rearrange("p (e h) -> p e h", e=E),
                         W1[:, P:2 * P, :].rearrange("e p h -> p e h")).then_inc(s_w1_in, 16)
            sp.dma_start(wg_raw, Wg).then_inc(s_wg_in, 16)
            sp.wait_ge(s_cleared, 1)
            for i in range(3):
                sp.dma_start(b2_raw[32 * i:32 * i + E, :], b2).then_inc(s_b2_in, 16)
            sp.dma_start(w2_sb[:, :, :], W2.rearrange("e h d -> (e h) d").rearrange("(m p) d -> p m d", p=P)
                         ).then_inc(s_w2_in, 16)
            sp.wait_ge(s_cleared, 2)
            sp.wait_ge(s_dve_setup, 4)
            for i in range(4):
                part, rows = i // 2, slice(64 * (i % 2), 64 * (i % 2) + 64)
                sp.dma_start(gray_halo_dram[part, rows, :], (halo_hi, halo_lo)[part][rows, :].bitcast(F32)
                             ).then_inc(stored[i], 16)
            for i in range(4):
                sp.wait_ge(stored[i], 16)
            sp.wait_ge(s_built, 1)

            def step(at):
                if at.has(GRAY):
                    b = at.buf(GRAY)
                    sp.wait_ge(s_gray, at.count(GRAY, 1, 1, back=2))
                    load_planes(at.j, at.u, b)
                    sp.wait_ge(s_edge_ps, at.count(GRAY, 4, 4, back=1))
                    for i, part in enumerate((0, 0, 1)):
                        row = at.j * (UNROLL * 4) + 4 * at.u
                        src = bass.AP(gray_halo_dram.tensor, part * P * (D + 2) + row * (D + 2),
                                      [[1, 3], [D + 2, 4], [1, D]])
                        dst = halo[32 * i:32 * i + 3, :, :, :].bitcast(F32).rearrange("p i r w -> p (i r) w")
                        sp.dma_start(dst, src).then_inc(halo_in, 16)
                if at.has(FFN):
                    b = at.buf(FFN, 4)
                    for half in range(HALF):
                        sp.wait_ge(s_result, at.results(half + 1))
                        first = at.j * (UNROLL * 2) + 2 * (at.u - FFN)
                        dst = out[bass.ds(first, 2), half * P:(half + 1) * P, :].rearrange("n p w -> p n w")
                        sp.dma_start(dst, edge[b][:, 2 * half:2 * half + 2, :]).then_inc(stored[b], 16)

            run_steps(sp, step)
            for i in range(4):
                sp.wait_ge(stored[i], 16 + 16 * HALF * PAIRS // 4)

        @block.gpsimd
        def _(pool):
            pool.memset(b2_raw, 0.0).then_inc(s_cleared, 1)
            for t in (halo_hi, halo_lo):
                pool.memset(t[:, 0:1].bitcast(F32), 0.0)
                pool.memset(t[:, D + 1:D + 2].bitcast(F32), 0.0)
            pool.memset(shift, 0.0).then_inc(s_cleared, 1)
            pool.wait_ge(s_cleared, 2)
            for di in range(3):
                pool.affine_select(out=shift[:, di, :], in_=shift[:, di, :], compare_op=ALU.not_equal, fill=1.0,
                                   base=1 - di, pattern=[[-1, P]], channel_multiplier=1).then_inc(s_cleared, 1)
            pool.memset(mask_rows[:, :], MASK_OUT).then_inc(s_cleared, 1)
            pool.wait_ge(s_cleared, 6)
            pool.affine_select(out=mask_rows[:, :], in_=mask_rows[:, :], compare_op=ALU.is_ge, fill=0.0,
                               base=96 * H, pattern=[[1, E * H]], channel_multiplier=-H).then_inc(s_cleared, 1)
            pool.wait_ge(s_cleared, 7)
            pool.affine_select(out=mask_rows[:, :], in_=mask_rows[:, :], compare_op=ALU.is_ge, fill=0.0,
                               base=H - 1 - 96 * H, pattern=[[-1, E * H]], channel_multiplier=H).then_inc(s_cleared, 1)
            pool.memset(halo[:, :, :, :].bitcast(F32), 0.0)
            for g in (gray_hi, gray_lo):
                pool.memset(g[:, :, 0:1].bitcast(F32), 0.0)
                pool.memset(g[:, :, D + 1:D + 2].bitcast(F32), 0.0)
            pool.memset(normed_t[:, :, 0:1], 0.0)
            pool.memset(k_pad[:, :, 0:1], NEVER)
            for t in (fresh, decay, fresh_v):
                pool.memset(t[:, :, 0:1], 0.0)
            for e in range(E):
                pool.memset(descending[:, e:e + 1], float(E - e))
            pool.memset(cap[:, :], BONUS_CAP)
            pool.memset(eps[:, 0:1], LN_EPS)
            pool.memset(eps[:, 1:2], LN_EPS * LN_EPS)
            pool.memset(band_halo[:, :, :].bitcast(F32), 0.0)
            pool.memset(b2_parts[:, :], 0.0)
            pool.memset(route[:, :, :], 0.0).then_inc(s_built, 1)

        @block.vector
        def _(dve):
            own = [0]

            def done(ins):
                own[0] += 1
                ins.then_inc(s_dve_setup, 1)
                dve.wait_ge(s_dve_setup, own[0])

            dve.wait_ge(s_halo_planes_in, 48)
            done(dve.tensor_scalar(halo_gray, halo_planes[:, 0, :], GRAY_WEIGHTS[0], None, ALU.mult))
            for i in (1, 2):
                done(dve.scalar_tensor_tensor(out=halo_gray, in0=halo_planes[:, i, :], scalar=GRAY_WEIGHTS[i],
                                              in1=halo_gray, op0=ALU.mult, op1=ALU.add))
            dve.wait_ge(s_act_setup, 1)
            done(dve.tensor_tensor(halo_lo[:, 1:D + 1], halo_gray, halo_hi[:, 1:D + 1].bitcast(F32), ALU.subtract))

            dve.wait_ge(s_scharr_in, 16)
            dve.wait_ge(s_scharr_dj_in, 48)
            dve.wait_ge(s_cleared, 5)
            done(dve.tensor_scalar(scharr_all[:, :], scharr_all[:, :], 0.5, None, ALU.mult))
            for i in range(3):
                rows = slice(32 * i, 32 * i + 3)
                dve.tensor_scalar(scharr_dj[rows, :], scharr_dj[rows, :], 0.5, None, ALU.mult)
            done(dve.tensor_copy(ident[:, :], shift[:, 1, :]))
            for i in range(3):
                rows = slice(32 * i, 32 * i + 3)
                dve.tensor_copy(scharr_hi[rows, :], scharr_dj[rows, :])
            done(dve.tensor_copy(ident_bf[:, :], ident[:, :]))
            for i in range(3):
                rows = slice(32 * i, 32 * i + 3)
                dve.tensor_tensor(scharr_lo[rows, :], scharr_dj[rows, :], scharr_hi[rows, :].bitcast(F32),
                                  ALU.subtract)
            for di in range(3):
                for c in range(2):
                    for dj in range(3):
                        weight = scharr_all[:, 9 * c + 3 * di + dj:9 * c + 3 * di + dj + 1]
                        b = band[:, 3 * c + dj, :]
                        if di == 0:
                            ins = dve.tensor_scalar(b, shift[:, di, :], weight, None, ALU.mult)
                        else:
                            ins = dve.scalar_tensor_tensor(out=b, in0=shift[:, di, :], scalar=weight, in1=b,
                                                           op0=ALU.mult, op1=ALU.add)
                done(ins)
            done(dve.tensor_copy(band_hi[:, :, :], band))
            done(dve.tensor_tensor(band_lo[:, :, :], band, band_hi[:, :, :].bitcast(F32), ALU.subtract))
            dve.wait_ge(s_built, 1)
            for half, (col, di) in enumerate(((P - 1, 2), (0, 0))):
                for c in range(2):
                    for i, part in enumerate((scharr_hi, scharr_lo, scharr_hi)):
                        rows = slice(32 * i, 32 * i + 3)
                        dve.tensor_copy(band_halo[rows, 2 * half + c, col:col + 1],
                                        part[rows, 3 * c + di:3 * c + di + 1].bitcast(F32))
            dve.wait_ge(s_pe_setup, 1)
            done(dve.tensor_copy(params[:, :], bank[0][:, 0:ROWS]))
            dve.tensor_scalar(cap_less_u[:, :], params[:, ROW_U:ROW_U + CH], -1.0, BONUS_CAP, ALU.mult, ALU.add)
            dve.memset(decay_step[:, :, 1:T + 1], -1.0)
            done(dve.memset(decay_step[:, :, 0:1], NEVER))
            dve.wait_ge(s_act_setup, 2)
            for ct in range(CH):
                seg = decay_step[:, 2 * ct:2 * ct + 2, 1:T + 1]
                done(dve.tensor_scalar(seg, seg, exp_w[:, ct:ct + 1], None, ALU.mult))
            dve.wait_ge(s_w1_in, 32)
            for ct in range(CH):
                cols = params[:, ROW_SCALE + ct:ROW_BIAS:CH]
                done(dve.tensor_tensor(w1_scaled[:, ct, :].rearrange("p (e h) -> p e h", e=E),
                                       w1_raw[:, ct, :].rearrange("p (e h) -> p e h", e=E),
                                       cols.unsqueeze(2).to_broadcast([P, E, H]), ALU.mult))
            done(dve.tensor_copy(w1_hi[:, :, :], w1_scaled))
            done(dve.tensor_tensor(w1_lo[:, :, :], w1_scaled, w1_hi[:, :, :].bitcast(F32), ALU.subtract))
            dve.wait_ge(s_b2_in, 48)
            b2_high = b2_parts[:, :]
            done(dve.tensor_copy(b2_mid, b2_raw))
            done(dve.tensor_tensor(b2_rest, b2_raw, b2_mid, ALU.subtract))
            done(dve.tensor_copy(b2_high[0:E, :], b2_mid[0:E, :]))
            done(dve.tensor_copy(b2_mid, b2_rest))
            done(dve.tensor_copy(b2_high[32:32 + E, :], b2_mid[32:32 + E, :]))
            done(dve.tensor_tensor(b2_rest, b2_rest, b2_mid, ALU.subtract))
            done(dve.tensor_copy(b2_high[64:64 + E, :], b2_rest[64:64 + E, :]))
            dve.wait_ge(s_pe_setup, 3)
            for i in range(4):
                dve.tensor_scalar(w_t[i][:, :, :].rearrange("p a d -> p (a d)"), bank[1 + i][:, :],
                                  0.5 if i == 3 else 1.0, None, ALU.mult)
            wg_t = bank[5][:, 0:CH * E].rearrange("p (c e) -> p c e", c=CH)
            done(dve.tensor_copy(wg_parts[:, :, 0:E], wg_t))
            dve.tensor_tensor(wg_parts[:, :, E:2 * E], wg_t, wg_parts[:, :, 0:E].bitcast(F32), ALU.subtract)
            dve.wait_ge(s_pe_setup, 4)
            for m in range(NM):
                for i in range(2):
                    rows = slice(64 * i, 64 * i + 64)
                    col = m * E + 2 * m + i
                    ins = dve.tensor_tensor(b1_full[rows, m:m + 1], bank[6][rows, col:col + 1],
                                            params[rows, ROW_B1 + m:ROW_B1 + m + 1], ALU.add)
            done(ins)
            dve.tensor_copy(best[:, 0:1], cap[:, :]).then_inc(s_result, RESULTS_AHEAD)

            def layer_norm_moments(i, src):
                for b in range(NB):
                    ins = dve.bn_stats(stats[i][:, b, :], src[:, b, :])
                ins.then_inc(s_stats[i], 1)

            def aggregate(i):
                for b in range(NB):
                    ins = dve.bn_aggr(moments[i][:, b, :], stats[i][:, b, :])
                ins.then_inc(s_moments[i], 1)

            def residual(half, at):
                dve.wait_ge(s_wo_ps, at.count(PROJ, 2, half + 1))
                dve.tensor_tensor(resid[at.buf(PROJ)][:, 2 * half:2 * half + 2, :], pair_view(bank[BANK_WO[half]]),
                                  edge[at.buf(PROJ, 4)][:, 2 * half:2 * half + 2, :], ALU.add
                                  ).then_inc(s_resid, 1)

            def normalise(i, stage, src, dst, at):
                dve.wait_ge(s_rstd[i], at.count(stage, 1, 1))
                for b in range(NB):
                    ins = dve.tensor_scalar(dst[:, b, :], src[:, b, :], moments[i][:, b, 0:1], rstd[i][:, b:b + 1],
                                            ALU.subtract, ALU.mult)
                ins.then_inc(s_normed_i[i], 1)

            def edge_sum(half, at):
                dve.wait_ge(s_abs, at.count(EDGE, 4, 2 * half + 2))
                hh = edge[at.buf(EDGE, 4)][:, 2 * half:2 * half + 2, :].rearrange("p i w -> p (i w)")
                dve.tensor_tensor(hh, hh, abs_a[:, half, :], ALU.add).then_inc(s_edge, 1)

            def step(at):
                if at.has(FFN):
                    dve.wait_ge(s_logits, at.count(FFN, 1, 1))
                    dve.tensor_reduce(logits[:, :, :], logits_parts.rearrange("p b (n e) -> p b e n", n=2),
                                      AXIS_X, ALU.add).then_inc(s_logits_sum, 1)
                    dve.wait_ge(s_logits_sum, at.count(FFN, 1, 1))
                    dve.tensor_reduce(best[:, :], logits[:, :, :], AXIS_X, ALU.max).then_inc(s_best, 1)
                    dve.wait_ge(s_best, at.count(FFN, 1, 1))
                    dve.tensor_tensor(rank[:, :, :], logits[:, :, :],
                                      best[:, :].unsqueeze(2).to_broadcast([P, NB, E]),
                                      ALU.is_equal).then_inc(s_hits, 1)
                    dve.wait_ge(s_hits, at.count(FFN, 1, 1))
                    dve.tensor_tensor(rank[:, :, :], rank[:, :, :],
                                      descending[:, :].unsqueeze(1).to_broadcast([P, NB, E]), ALU.mult
                                      ).then_inc(s_ranked, 1)
                    dve.wait_ge(s_ranked, at.count(FFN, 1, 1))
                    dve.tensor_reduce(best_rank[:, :], rank[:, :, :], AXIS_X, ALU.max).then_inc(s_best_rank, 1)
                    dve.wait_ge(s_best_rank, at.count(FFN, 1, 1))
                    groups = route[:, :, :].rearrange("p b (g e) -> p b g e", g=4)
                    dve.tensor_tensor(groups[:, :, 0:3, 0:E], rank[:, :, :].unsqueeze(2).to_broadcast([P, NB, 3, E]),
                                      best_rank[:, :].unsqueeze(2).unsqueeze(3).to_broadcast([P, NB, 3, E]),
                                      ALU.is_equal)
                    dve.tensor_tensor(groups[:, :, 3, 0:E], rank[:, :, :],
                                      best_rank[:, :].unsqueeze(2).to_broadcast([P, NB, E]),
                                      ALU.not_equal).then_inc(s_route, 1)
                if at.has(EDGE):
                    edge_sum(0, at)
                if at.has(GRAY):
                    b = at.buf(GRAY)
                    dve.wait_ge(s_red, at.count(GRAY, 1, 1))
                    dve.scalar_tensor_tensor(out=gray[:, :, :], in0=planes[b][:, :, 1, :], scalar=GRAY_WEIGHTS[1],
                                             in1=gray[:, :, :], op0=ALU.mult, op1=ALU.add).then_inc(s_red_green, 1)
                if at.has(EDGE):
                    edge_sum(1, at)
                    dve.wait_ge(s_edge, at.count(EDGE, 2, 2))
                    layer_norm_moments(0, edge[at.buf(EDGE, 4)])
                    dve.wait_ge(s_stats[0], at.count(EDGE, 1, 1))
                if at.has(GRAY):
                    dve.wait_ge(s_red_green, at.count(GRAY, 1, 1))
                    dve.scalar_tensor_tensor(out=gray[:, :, :], in0=planes[b][:, :, 2, :], scalar=GRAY_WEIGHTS[2],
                                             in1=gray[:, :, :], op0=ALU.mult, op1=ALU.add).then_inc(s_gray, 1)
                if at.has(EDGE):
                    aggregate(0)
                if at.has(WKV):
                    dve.wait_ge(s_k, at.count(WKV, 2, 2))
                    dve.tensor_tensor_scan(flat(max_num), flat(decay_step), flat(k_pad), 0.0,
                                           ALU.add, ALU.max).then_inc(s_max, 1)
                    dve.wait_ge(s_max, at.count(WKV, 1, 1))
                    dve.tensor_tensor(k_pad[:, :, 1:T + 1], k_pad[:, :, 1:T + 1], max_num[:, :, 0:T],
                                      ALU.subtract).then_inc(s_gap, 1)
                    dve.wait_ge(s_gap, at.count(WKV, 1, 1))
                    gap = k_pad[:, :, 1:T + 1]
                    for ct in range(CH):
                        seg = slice(2 * ct, 2 * ct + 2)
                        ins = dve.tensor_scalar(fresh[:, seg, 1:T + 1], gap[:, seg, :], exp_w[:, ct:ct + 1], 0.0,
                                                ALU.add, ALU.min)
                    ins.then_inc(s_exponents, 1)
                if at.has(PROJ):
                    dve.wait_ge(s_result, at.results(2, back=1))
                    residual(0, at)
                    residual(1, at)
                    dve.wait_ge(s_resid, at.count(PROJ, 2, 2))
                    layer_norm_moments(1, resid[at.buf(PROJ)])
                    dve.wait_ge(s_stats[1], at.count(PROJ, 1, 1))
                if at.has(GRAY):
                    dve.wait_ge(s_gray_hi, at.count(GRAY, 1, 1))
                    dve.tensor_tensor(gray_lo[:, :, 1:D + 1], gray[:, :, :], gray_hi[:, :, 1:D + 1].bitcast(F32),
                                      ALU.subtract).then_inc(s_gray_lo, 1)
                if at.has(PROJ):
                    aggregate(1)
                if at.has(EDGE):
                    dve.wait_ge(s_normed_ps, at.count(EDGE, 2, 2, back=1))
                    dve.wait_ge(s_mixed, at.count(EDGE, 3, 3, back=1))
                    normalise(0, EDGE, edge[at.buf(EDGE, 4)], normed, at)
                if at.has(PROJ):
                    dve.wait_ge(s_normed2_ps, at.count(PROJ, 2, 2, back=1))
                    normalise(1, PROJ, resid[at.buf(PROJ)], normed2, at)
                if at.has(WKV):
                    dve.wait_ge(s_exps, at.count(WKV, 3, 2))
                    dve.tensor_tensor_scan(flat(den_state), flat(decay), flat(fresh), 0.0,
                                           ALU.mult, ALU.add).then_inc(s_den_state, 1)
                    dve.wait_ge(s_v, at.count(WKV, 2, 2))
                    dve.tensor_tensor(fresh_v[:, :, 1:T + 1], fresh[:, :, 1:T + 1], v_sb[:, :, :],
                                      ALU.mult).then_inc(s_fresh_v, 1)
                    dve.wait_ge(s_exps, at.count(WKV, 3, 3))
                    dve.wait_ge(s_den_state, at.count(WKV, 1, 1))
                    dve.tensor_tensor(den[:, :, :], bonus[:, :, :], den_state[:, :, 0:T],
                                      ALU.add).then_inc(s_den, 1)
                    dve.tensor_tensor(bonus[:, :, :], bonus[:, :, :], v_sb[:, :, :], ALU.mult
                                      ).then_inc(s_bonus_v, 1)
                    dve.wait_ge(s_fresh_v, at.count(WKV, 1, 1))
                    dve.tensor_tensor_scan(flat(max_num), flat(decay), flat(fresh_v), 0.0,
                                           ALU.mult, ALU.add).then_inc(s_num_state, 1)
                    dve.wait_ge(s_num_state, at.count(WKV, 1, 1))
                    dve.wait_ge(s_bonus_v, at.count(WKV, 1, 1))
                    dve.tensor_tensor(bonus[:, :, :], bonus[:, :, :], max_num[:, :, 0:T], ALU.add
                                      ).then_inc(s_num, 1)
                if at.has(PROJ):
                    dve.wait_ge(s_hidden_ps, at.count(FFN, 4, 4))
                    for ct in range(CH):
                        dve.wait_ge(s_normed2_hi, at.count(PROJ, 2, ct + 1))
                        dve.tensor_tensor(normed2_lo[:, ct, :, :], pair_view(bank[BANK_NORMED2[ct]]),
                                          normed2_hi[:, ct, :, :].bitcast(F32), ALU.subtract
                                          ).then_inc(s_normed2_lo, 1)
                if at.has(WKV):
                    dve.wait_ge(s_num, at.count(WKV, 1, 1))
                    dve.wait_ge(s_gate, at.count(WKV, 2, 2))
                    dve.scalar_tensor_tensor(out=bonus[:, :, :], in0=gate[:, :, :], scalar=1.0, in1=bonus[:, :, :],
                                             op0=ALU.add, op1=ALU.mult).then_inc(s_gated, 1)
                if at.has(FFN):
                    dve.wait_ge(s_resid, at.count(FFN, 2, 2))
                    for half in range(HALF):
                        dve.wait_ge(s_y_ps, at.count(FFN, 2, half + 1))
                        dve.tensor_tensor(edge[at.buf(FFN, 4)][:, 2 * half:2 * half + 2, :],
                                          pair_view(bank[BANK_Y[half]]), resid[at.buf(FFN)][:, 2 * half:2 * half + 2, :],
                                          ALU.add).then_inc(s_result, 1)
                if at.has(WKV):
                    dve.wait_ge(s_gated, at.count(WKV, 1, 1))
                    dve.wait_ge(s_recip, at.count(WKV, 1, 1))
                    dve.wait_ge(s_wo_ps, at.count(PROJ, 2, 2))
                    dve.tensor_tensor(rwkv[:, :, :], bonus[:, :, :], den[:, :, :], ALU.mult).then_inc(s_rwkv, 1)
                if at.has(EDGE):
                    dve.wait_ge(s_normed_t, at.count(EDGE, 2, 2))
                    dve.tensor_tensor(step_diff[:, :, :], normed_t[:, :, 1:T + 1], normed_t[:, :, 0:T],
                                      ALU.subtract).then_inc(s_diff, 1)
                    dve.wait_ge(s_diff, at.count(EDGE, 1, 1))
                    for i in range(3):
                        dve.wait_ge(s_proj_ps, at.count(EDGE, 6, 2 * i + 2, back=1))
                        for ct in range(CH):
                            seg = slice(2 * ct, 2 * ct + 2)
                            ins = dve.scalar_tensor_tensor(
                                out=mixed[i][:, seg, :], in0=step_diff[:, seg, :],
                                scalar=params[:, ROW_TM[i] + ct:ROW_TM[i] + ct + 1],
                                in1=normed_t[:, seg, 0:T], op0=ALU.mult, op1=ALU.add)
                        ins.then_inc(s_mixed, 1)

            def flat(t):
                return t[:, :, :].rearrange("p s t -> p (s t)")

            def pair_view(ps):
                return ps[:, :].rearrange("p (i w) -> p i w", i=2)

            run_steps(dve, step)

        @block.scalar
        def _(act):
            act.wait_ge(s_dve_setup, 3)
            act.activation(halo_hi[:, 1:D + 1], halo_gray, ACT.Copy).then_inc(s_act_setup, 1)
            act.wait_ge(s_dve_setup, 13)
            act.activation(exp_w[:, :], params[:, ROW_W:ROW_W + CH], ACT.Exp).then_inc(s_act_setup, 1)

            def reciprocal_std(i, stage, at):
                act.wait_ge(s_moments[i], at.count(stage, 1, 1))
                act.activation(log_var[i][:, :], moments[i][:, :, 1], ACT.Ln, bias=eps[:, i:i + 1],
                               scale=1.0 if i == 0 else 1.0 + LN_EPS).then_inc(s_log_var[i], 1)
                act.wait_ge(s_log_var[i], at.count(stage, 1, 1))
                act.activation(rstd[i][:, :], log_var[i][:, :], ACT.Exp, scale=-0.5).then_inc(s_rstd[i], 1)

            def absolute(half, at):
                b = at.buf(EDGE, 4)
                act.wait_ge(s_edge, at.count(EDGE, 2, half + 1, back=1))
                act.wait_ge(stored[b], 16 + at.dma_count(FFN, 2, n=4, back=1))
                for c, dst in enumerate((abs_a[:, half, :], edge[b][:, 2 * half:2 * half + 2, :]
                                         .rearrange("p i w -> p (i w)"))):
                    act.wait_ge(s_edge_ps, at.count(EDGE, 4, 2 * half + c + 1))
                    act.activation(dst, bank[BANK_EDGE[2 * half + c]][:, :], ACT.Abs).then_inc(s_abs, 1)

            def step(at):
                if at.u == 0:
                    act.preload_act_table_set("natural_log_exp_and_others")
                if at.has(EDGE):
                    absolute(0, at)
                if at.has(GRAY):
                    b = at.buf(GRAY)
                    act.wait_ge(planes_in[b], at.dma_count(GRAY, 2))
                    act.wait_ge(s_gray_lo, at.count(GRAY, 1, 1, back=1))
                    act.activation(gray[:, :, :], planes[b][:, :, 0, :], ACT.Copy, scale=GRAY_WEIGHTS[0]
                                   ).then_inc(s_red, 1)
                if at.has(EDGE):
                    absolute(1, at)
                if at.has(GRAY):
                    act.wait_ge(s_gray, at.count(GRAY, 1, 1))
                    act.wait_ge(s_edge_ps, at.count(GRAY, 4, 4, back=1))
                    act.activation(gray_hi[:, :, 1:D + 1], gray[:, :, :], ACT.Copy).then_inc(s_gray_hi, 1)
                if at.has(EDGE):
                    reciprocal_std(0, EDGE, at)
                if at.has(WKV):
                    act.wait_ge(s_exponents, at.count(WKV, 1, 1, back=1))
                    act.wait_ge(s_cap_arg, at.count(WKV, 1, 1, back=1))
                    copy_k(0, at)
                    copy_k(1, at)
                    act.wait_ge(s_bonus_v, at.count(WKV, 1, 1, back=1))
                    copy_v(0, at)
                    copy_v(1, at)
                    gap = k_pad[:, :, 1:T + 1]
                    act.wait_ge(s_gap, at.count(WKV, 1, 1))
                    act.wait_ge(s_num_state, at.count(WKV, 1, 1, back=1))
                    for ct in range(CH):
                        seg = slice(2 * ct, 2 * ct + 2)
                        ins = act.activation(decay[:, seg, 1:T + 1], gap[:, seg, :], ACT.Relu,
                                             bias=exp_w[:, ct:ct + 1])
                    ins.then_inc(s_decay_arg, 1)
                    act.wait_ge(s_rwkv, at.count(WKV, 1, 1, back=1))
                    for ct in range(CH):
                        seg = slice(2 * ct, 2 * ct + 2)
                        ins = act.activation(bonus[:, seg, :], gap[:, seg, :], ACT.Relu,
                                             bias=cap_less_u[:, ct:ct + 1], scale=-1.0)
                    ins.then_inc(s_cap_arg, 1)
                if at.has(FFN):
                    act.wait_ge(s_route_ps, at.count(FFN, 1, 1))
                    act.activation(route_t[:, :, :].rearrange("p i t -> p (i t)"), route_ps, ACT.Copy
                                   ).then_inc(s_route_t, 1)
                if at.has(WKV):
                    act.wait_ge(s_exponents, at.count(WKV, 1, 1))
                    act.activation(fresh[:, :, 1:T + 1], fresh[:, :, 1:T + 1], ACT.Exp).then_inc(s_exps, 1)
                    act.wait_ge(s_decay_arg, at.count(WKV, 1, 1))
                    act.activation(decay[:, :, 1:T + 1], decay[:, :, 1:T + 1], ACT.Exp, scale=-1.0
                                   ).then_inc(s_exps, 1)
                    act.wait_ge(s_cap_arg, at.count(WKV, 1, 1))
                    act.activation(bonus[:, :, :], bonus[:, :, :], ACT.Exp, bias=cap[:, :], scale=-1.0
                                   ).then_inc(s_exps, 1)
                if at.has(PROJ):
                    reciprocal_std(1, PROJ, at)
                if at.has(FFN):
                    for m in range(NM):
                        act.wait_ge(s_hidden_ps, at.count(FFN, 4, m + 1))
                        act.activation(hidden[:, m, :, :], pair_view(bank[BANK_HIDDEN[m]]), ACT.Gelu,
                                       bias=b1_full[:, m:m + 1]).then_inc(s_hidden, 1)
                if at.has(WKV):
                    act.wait_ge(s_gated, at.count(WKV, 1, 1, back=1))
                    gate_of(0, at)
                if at.has(PROJ):
                    act.wait_ge(s_hidden_ps, at.count(FFN, 4, 4))
                    for ct in range(CH):
                        act.wait_ge(s_normed2_ps, at.count(PROJ, 2, ct + 1))
                        act.activation(normed2_hi[:, ct, :, :], pair_view(bank[BANK_NORMED2[ct]]), ACT.Copy
                                       ).then_inc(s_normed2_hi, 1)
                if at.has(WKV):
                    gate_of(1, at)
                    act.preload_act_table_set("natural_log_exp_and_others")
                    act.wait_ge(s_den, at.count(WKV, 1, 1))
                    act.activation(den[:, :, :], den[:, :, :], ACT.Ln).then_inc(s_log_den, 1)
                    act.wait_ge(s_log_den, at.count(WKV, 1, 1))
                    act.activation(den[:, :, :], den[:, :, :], ACT.Exp, scale=-1.0).then_inc(s_recip, 1)
                if at.has(EDGE):
                    act.wait_ge(s_mixed, at.count(EDGE, 3, 3, back=1))
                    for ct in range(CH):
                        act.wait_ge(s_normed_ps, at.count(EDGE, 2, ct + 1))
                        act.activation(normed_t[:, 2 * ct:2 * ct + 2, 1:T + 1], pair_view(bank[BANK_NORMED[ct]]),
                                       ACT.Copy).then_inc(s_normed_t, 1)

            def copy_k(ct, at):
                act.wait_ge(s_proj_ps, at.count(WKV, 6, 1 + ct))
                act.activation(k_pad[:, 2 * ct:2 * ct + 2, 1:T + 1], pair_view(bank[BANK_K[ct]]), ACT.Copy
                               ).then_inc(s_k, 1)

            def gate_of(ct, at):
                act.wait_ge(s_proj_ps, at.count(WKV, 6, 5 + ct))
                act.activation(gate[:, 2 * ct:2 * ct + 2, :], pair_view(bank[BANK_R[ct]]), ACT.Tanh, scale=0.5
                               ).then_inc(s_gate, 1)

            def copy_v(ct, at):
                act.wait_ge(s_proj_ps, at.count(WKV, 6, 3 + ct))
                act.activation(v_sb[:, 2 * ct:2 * ct + 2, :], pair_view(bank[BANK_V[ct]]), ACT.Copy
                               ).then_inc(s_v, 1)

            def pair_view(ps):
                return ps[:, :].rearrange("p (i w) -> p i w", i=2)

            act.wait_ge(s_dve_setup, SETUP_OPS)
            run_steps(act, step)

        @block.tensor
        def _(pe):
            pe.wait_ge(s_dve_setup, 6)
            pe.wait_ge(s_params_in, 16 * 8)
            pe.transpose(bank[0][:, 0:ROWS], params_raw, ident[0:ROWS, 0:ROWS]).then_inc(s_pe_setup, 1)
            pe.wait_ge(s_w_in, 64)
            for i in range(4):
                for ct in range(CH):
                    for dt in range(CH):
                        ins = pe.transpose(bank[1 + i][:, ct * D + dt * P:ct * D + (dt + 1) * P],
                                           w_raw[i][:, dt, ct * P:(ct + 1) * P], ident[:, :])
            ins.then_inc(s_pe_setup, 1)
            pe.wait_ge(s_wg_in, 16)
            for ct in range(CH):
                ins = pe.transpose(bank[5][:, ct * E:(ct + 1) * E], wg_raw[:, ct * P:(ct + 1) * P], ident[0:E, 0:E])
            ins.then_inc(s_pe_setup, 1)
            pe.wait_ge(s_w1_in, 32)
            pe.wait_ge(s_dve_setup, 13)
            for m in range(NM):
                for ct in range(CH):
                    ins = pe.matmul(bank[6][:, m * E:(m + 1) * E], w1_raw[:, ct, m * P:(m + 1) * P],
                                    params[:, ROW_BIAS + ct:ROW_B1:CH], start=(ct == 0), stop=(ct == CH - 1))
            ins.then_inc(s_pe_setup, 1)
            pe.wait_ge(s_w2_in, 16)
            pe.wait_ge(s_dve_setup, SETUP_OPS)
            pe.wait_ge(s_cleared, 8)

            def project(at, i, ct, dst):
                for kt in range(CH):
                    ins = pe.matmul(dst[:, :], w_t[i][:, kt, ct * P:(ct + 1) * P],
                                    mixed[i][:, 2 * kt:2 * kt + 2, :].rearrange("p i t -> p (i t)"),
                                    start=(kt == 0), stop=(kt == CH - 1))
                ins.then_inc(s_proj_ps, 1)

            def step(at):
                if at.has(EDGE):
                    pe.wait_ge(s_gray_lo, at.count(EDGE, 1, 1))
                    pe.wait_ge(halo_in, at.count(EDGE, 48, 48))
                    for n in range(2 * HALF):
                        half, c = divmod(n, 2)
                        if n == 0:
                            pe.wait_ge(s_gate, at.count(WKV, 2, 2, back=1))
                        elif n < 3:
                            pe.wait_ge(s_normed2_lo, at.count(PROJ, 2, n, back=1))
                        else:
                            pe.wait_ge(s_result, at.results(1, back=1))
                        ps = bank[BANK_EDGE[n]]
                        for dj in range(3):
                            for i, (weights, part) in enumerate(((band_hi, gray_hi), (band_lo, gray_hi),
                                                                 (band_hi, gray_lo))):
                                pe.matmul(ps[:, :], weights[:, 3 * c + dj, :],
                                          part[:, 2 * half:2 * half + 2, dj:dj + D],
                                          start=(dj == 0 and i == 0), stop=False)
                        pe.matmul(ps[:, :], band_halo[:, 2 * half + c, :], halo[:, :, 1 - half, :],
                                  start=False, stop=True).then_inc(s_edge_ps, 1)
                if at.has(WKV):
                    pe.wait_ge(s_mixed, at.count(WKV, 3, 1))
                    pe.wait_ge(s_normed_t, at.count(WKV, 2, 2))
                    project(at, 0, 0, bank[BANK_K[0]])
                    pe.wait_ge(s_gate, at.count(WKV, 2, 1, back=1))
                    if at.has(FFN):
                        pe.wait_ge(s_logits_sum, at.count(FFN, 1, 1))
                    project(at, 0, 1, bank[BANK_K[1]])
                    pe.wait_ge(s_mixed, at.count(WKV, 3, 2))
                    for ct in range(CH):
                        pe.wait_ge(s_abs, at.count(EDGE, 4, ct + 1))
                        project(at, 1, ct, bank[BANK_V[ct]])
                if at.has(PROJ):
                    pe.wait_ge(s_rwkv, at.count(PROJ, 1, 1))
                    pe.wait_ge(s_result, at.results(2, back=1))
                    output_projection(0, at)
                    pe.wait_ge(s_normed_t, at.count(EDGE, 2, 1, back=1))
                    output_projection(1, at)
                if at.has(FFN):
                    pe.wait_ge(s_route, at.count(FFN, 1, 1))
                    pe.wait_ge(s_abs, at.count(EDGE, 4, 3))
                    pe.wait_ge(s_normed2_lo, at.count(FFN, 2, 2))
                    for i in range(2):
                        for half in range(HALF):
                            col = i * T + half * P
                            ins = pe.transpose(route_ps[:, col:col + P], route[:, 2 * half + i, :], ident_bf[:, :])
                    ins.then_inc(s_route_ps, 1)
                    for m in range(NM):
                        ps = bank[BANK_HIDDEN[m]]
                        if m == 0:
                            pe.wait_ge(s_abs, at.count(EDGE, 4, 4))
                            pe.wait_ge(s_result, at.results(1, back=1))
                        elif m < 3:
                            pe.wait_ge(s_resid, at.count(PROJ, 2, m))
                        else:
                            pe.wait_ge(s_k, at.count(WKV, 2, 1))
                        for kt in range(CH):
                            for n, (weights, part) in enumerate(((w1_hi, normed2_hi), (w1_lo, normed2_hi),
                                                                 (w1_hi, normed2_lo))):
                                pe.matmul(ps[:, :], weights[:, kt, m * P:(m + 1) * P],
                                          part[:, kt, :, :].rearrange("p i t -> p (i t)"),
                                          start=(kt == 0 and n == 0), stop=False)
                        if m == 1:
                            pe.wait_ge(s_route_t, at.count(FFN, 1, 1))
                        for n in ([], [0, 1], [2], [3])[m]:
                            pe.matmul(bank[BANK_HIDDEN[n]][:, :], mask_rows[:, n * P:(n + 1) * P],
                                      route_t[:, :, :].rearrange("p i t -> p (i t)"),
                                      start=False, stop=True).then_inc(s_hidden_ps, 1)
                if at.has(WKV):
                    pe.wait_ge(s_mixed, at.count(WKV, 3, 3))
                    pe.wait_ge(s_k, at.count(WKV, 2, 2))
                    project(at, 2, 0, bank[BANK_R[0]])
                if at.has(PROJ):
                    pe.wait_ge(s_normed2, at.count(PROJ, 1, 1))
                    pe.wait_ge(s_v, at.count(WKV, 2, 2))
                    transposed(normed2, BANK_NORMED2[0], 0).then_inc(s_normed2_ps, 1)
                    if at.has(FFN):
                        pe.wait_ge(s_route_t, at.count(FFN, 1, 1))
                    else:
                        pe.wait_ge(s_abs, at.count(EDGE, 4, 4))
                    transposed(normed2, BANK_NORMED2[1], 1).then_inc(s_normed2_ps, 1)
                if at.has(WKV):
                    pe.wait_ge(s_v, at.count(WKV, 2, 1))
                    project(at, 2, 1, bank[BANK_R[1]])
                if at.has(FFN):
                    pe.wait_ge(s_hidden, at.count(FFN, 4, 4))
                    for half in range(HALF):
                        for i in range(2):
                            ps = bank[BANK_Y[half]][:, i * D:(i + 1) * D]
                            rows = slice(half * P, (half + 1) * P)
                            for m in range(NM):
                                pe.matmul(ps, hidden[:, m, i, rows], w2_sb[:, m, :], start=(m == 0), stop=False)
                            ins = pe.matmul(ps, route_t[:, i, rows], b2_parts[:, :], start=False, stop=True)
                        ins.then_inc(s_y_ps, 1)
                if at.has(EDGE):
                    pe.wait_ge(s_normed, at.count(EDGE, 1, 1))
                    if not at.has(FFN):
                        pe.wait_ge(s_k, at.count(WKV, 2, 1))
                        pe.wait_ge(s_resid, at.count(PROJ, 2, 2))
                    transposed(normed, BANK_NORMED[0], 0).then_inc(s_normed_ps, 1)
                    transposed(normed, BANK_NORMED[1], 1).then_inc(s_normed_ps, 1)
                if at.has(PROJ):
                    pe.wait_ge(s_normed2_lo, at.count(PROJ, 2, 2))
                    pe.wait_ge(s_gate, at.count(WKV, 2, 1))
                    for half in range(HALF):
                        for i in range(2):
                            rows = slice(half * P, (half + 1) * P)
                            for kt in range(CH):
                                for n, part in enumerate((normed2_hi, normed2_lo)):
                                    ins = pe.matmul(logits_parts[:, 2 * half + i, :], part[:, kt, i, rows],
                                                    wg_parts[:, kt, :],
                                                    start=(kt == 0 and n == 0), stop=(kt == CH - 1 and n == 1))
                    ins.then_inc(s_logits, 1)

            def transposed(src, n, ct):
                for i in range(2):
                    for half in range(HALF):
                        col = i * T + half * P
                        ins = pe.transpose(bank[n][:, col:col + P], src[:, 2 * half + i, ct * P:(ct + 1) * P],
                                           ident[:, :])
                return ins

            def output_projection(half, at):
                for i in range(2):
                    for kt in range(CH):
                        ins = pe.matmul(bank[BANK_WO[half]][:, i * D:(i + 1) * D],
                                        rwkv[:, 2 * kt + i, half * P:(half + 1) * P], w_t[3][:, kt, :],
                                        start=(kt == 0), stop=(kt == CH - 1))
                ins.then_inc(s_wo_ps, 1)

            run_steps(pe, step)


SETUP_OPS = 29


_INS = ['x', 'L0_tok_scharr', 'L0_attn_w', 'L0_attn_u', 'L0_attn_time_mix_k', 'L0_attn_time_mix_v',
        'L0_attn_time_mix_r', 'L0_attn_Wk', 'L0_attn_Wv', 'L0_attn_Wr', 'L0_attn_Wo', 'L0_ffn_Wg',
        'L0_ffn_ln_scale', 'L0_ffn_ln_bias', 'L0_ffn_W1', 'L0_ffn_b1', 'L0_ffn_W2', 'L0_ffn_b2']
_OUTS = [((64, 256, 256), 'float32')]


def kernel(**inputs):
    import numpy as _np
    import concourse.bacc as _bacc
    from concourse import mybir as _mybir
    from concourse.bass_utils import run_bass_kernel_spmd as _run

    nc = _bacc.Bacc("TRN2", target_bir_lowering=False, num_devices=1)
    arrays, args = {}, []
    for name in _INS:
        a = _np.ascontiguousarray(inputs[name])
        arrays[f"in_{name}_dram"] = a
        args.append(nc.dram_tensor(f"in_{name}_dram", a.shape, _mybir.dt.from_np(a.dtype), kind="ExternalInput").ap())
    for i, (shape, dtype) in enumerate(_OUTS):
        dt = _mybir.dt.from_np(_np.dtype(dtype))
        args.append(nc.dram_tensor(f"out_{i}_dram", shape, dt, kind="ExternalOutput").ap())
    vision_layer(nc, *args)
    r = _run(nc, [arrays], core_ids=[0])
    got = tuple(r.results[0][f"out_{i}_dram"] for i in range(len(_OUTS)))
    return got[0]
```

```python
import concourse.bass as bass
from concourse import mybir
from contextlib import ExitStack

F32 = mybir.dt.float32
F32R = mybir.dt.float32r
BF16 = mybir.dt.bfloat16
ALU = mybir.AluOpType
ACT = mybir.ActivationFunctionType
AXIS_X = mybir.AxisListType.X

GRAY_WEIGHTS = (0.2989, 0.587, 0.114)
LN_EPS = 1e-5
NEVER = -1e38
BONUS_CAP = 40.0
MASK_OUT = -float(2 ** 40)
GRAY, EDGE, WKV, PROJ, FFN = range(5)
RESULTS_AHEAD = 2
UNROLL = 4

SETUP_HALO_GRAY, SETUP_HALO, SETUP_IDENT, SETUP_PARAMS = 3, 4, 6, 14
SETUP_CONV, SETUP_PROJECTIONS, SETUP_EXPERTS, SETUP_ALL = 14, 21, 32, 36
CLEARED_B2, CLEARED_SHIFT, CLEARED_BUILT_SHIFT, CLEARED_MASK = 1, 2, 5, 8


class Step:

    def __init__(self, j, u, pairs):
        self.j, self.u, self.pairs = j, u, pairs

    def filling(self):
        return isinstance(self.j, int) and UNROLL * self.j + self.u < FFN

    def first(self):
        return isinstance(self.j, int) and UNROLL * self.j + self.u == 0

    def has(self, stage):
        return not isinstance(self.j, int) or 0 <= UNROLL * self.j + self.u - stage < self.pairs

    def buf(self, stage, n=2):
        return (self.u - stage) % n

    def count(self, stage, per_pair, k, back=0):
        v = self.j * (UNROLL * per_pair) + (per_pair * (self.u - stage - back) + k)
        return min(max(0, v), per_pair * self.pairs) if isinstance(v, int) else v

    def dma_count(self, stage, dmas, n=2, back=0):
        v = self.j * (UNROLL // n * 16 * dmas) + 16 * dmas * ((self.u - stage - back) // n + 1)
        return max(0, v) if isinstance(v, int) else v

    def results(self, k, back=0):
        return RESULTS_AHEAD + self.count(FFN, 2, k, back)


def vision_layer(nc, x, scharr, w, u, time_mix_k, time_mix_v, time_mix_r, Wk, Wv, Wr, Wo,
                 Wg, ln_scale, ln_bias, W1, b1, W2, b2, out):
    B, NCOL, T, D = x.shape
    E, _, H = W1.shape
    P = 128
    PAIRS = B // 2
    HALF = T // P
    CH = D // P
    NB = HALF * 2
    NM = E * H // P
    assert T == 256 and D == 256 and NCOL == 3 and E == 8 and E * H == 512
    assert PAIRS % UNROLL == 0 and PAIRS // UNROLL >= 2

    ROW_W, ROW_U, ROW_TM = 0, 2, (4, 6, 8)
    ROW_SCALE, ROW_BIAS, ROW_B1 = 10, 10 + E * CH, 10 + 2 * E * CH
    ROWS = ROW_B1 + NM

    x_planes = x.rearrange("n c h w -> (n c) h w")
    gray_halo_dram = nc.dram_tensor("gray_halo_dram", [2, P, D + 2], F32).ap()

    with ExitStack() as ctx:
        def sb(name, shape, dt=F32):
            return ctx.enter_context(nc.sbuf_tensor(name, shape, dt))

        def sem(name):
            return ctx.enter_context(nc.semaphore(name))

        planes = [sb(f"planes{i}", [P, NB, NCOL, D]) for i in range(2)]
        gray = sb("gray", [P, NB, D])
        gray_hi = sb("gray_hi", [P, NB, D + 2], F32R)
        gray_lo = sb("gray_lo", [P, NB, D + 2], F32R)
        halo = sb("halo", [P, 2, 2, D], F32R)
        edge = [sb(f"edge{i}", [P, NB, D]) for i in range(4)]
        normed = sb("normed", [P, NB, D])
        normed_t = sb("normed_t", [P, NB, T + 1])
        step_diff = normed
        mixed_hi, mixed_lo = [[sb(f"mixed_{n}_{part}", [P, NB, T], F32R) for n in "kvr"] for part in ("hi", "lo")]
        gap = sb("gap", [P, NB, T])
        v_sb = sb("v_sb", [P, NB, T])
        gate = sb("gate", [P, NB, T])
        max_state = sb("max_state", [P, NB, T + 1])
        den_state = sb("den_state", [P, NB, T + 1])
        num_state = sb("num_state", [P, NB, T + 1])
        fresh = sb("fresh", [P, NB, T + 1])
        decay = sb("decay", [P, NB, T + 1])
        bonus = sb("bonus", [P, NB, T])
        den = sb("den", [P, NB, T])
        abs_a = den[:, :, :].rearrange("p (h i) t -> p h (i t)", h=HALF)
        rwkv_hi, rwkv_lo = [sb(f"rwkv_{part}", [P, NB, T], F32R) for part in ("hi", "lo")]
        rwkv = bonus[:, :, :]
        mixed = (gap[:, :, :], v_sb[:, :, :], gate[:, :, :])
        resid = [sb(f"resid{i}", [P, NB, D]) for i in range(2)]
        normed2 = sb("normed2", [P, NB, D])
        normed2_hi = sb("normed2_hi", [P, CH, 2, T], F32R)
        normed2_lo = sb("normed2_lo", [P, CH, 2, T], F32R)
        route = sb("route", [P, NB, P], BF16)
        route_t = sb("route_t", [P, 2, T], BF16)
        hidden = sb("hidden", [P, NM, 2, T])
        stats = [sb(f"stats{i}", [P, NB, 6]) for i in range(2)]
        moments = [sb(f"moments{i}", [P, NB, 2]) for i in range(2)]
        log_var = [sb(f"log_var{i}", [P, NB]) for i in range(2)]
        rstd = [sb(f"rstd{i}", [P, NB]) for i in range(2)]
        logits = sb("logits", [P, NB, E])
        neg_shift = sb("neg_shift", [P, NB])
        best = sb("best", [P, NB])
        rank = sb("rank", [P, NB, E])
        best_rank = sb("best_rank", [P, NB])

        ident = sb("ident", [P, P])
        ident_bf = sb("ident_bf", [P, P], BF16)
        band_hi = sb("band_hi", [P, 6, P], F32R)
        band_lo = sb("band_lo", [P, 6, P], F32R)
        band_halo = sb("band_halo", [P, 2 * HALF, P], F32R)
        params = sb("params", [P, ROWS])
        w_hi, w_lo = [[sb(f"w_{n}_{p}", [P, CH, D], F32R) for n in "kvro"] for p in ("hi", "lo")]
        wg_parts = sb("wg_parts", [P, CH, 2 * E], F32R)
        w1_hi, w1_lo = [sb(f"w1_{n}", [P, CH, E * H], F32R) for n in ("hi", "lo")]
        b1_full = sb("b1_full", [P, NM])
        w2_sb = sb("w2_sb", [P, NM, D])
        b2_parts = sb("b2_parts", [P, D], BF16)
        mask_rows = sb("mask_rows", [P, E * H], BF16)
        exp_w = sb("exp_w", [P, CH])
        neg_exp_w = sb("neg_exp_w", [P, CH])
        cap_less_u = sb("cap_less_u", [P, CH])
        cap = sb("cap", [P, 1])
        eps = sb("eps", [P, 2])
        descending = sb("descending", [P, E])
        scharr_all = sb("scharr_all", [P, 18])
        scharr_dj = sb("scharr_dj", [P, 6])
        scharr_hi = sb("scharr_hi", [P, 6], F32R)
        scharr_lo = sb("scharr_lo", [P, 6], F32R)

        w_raw = [(gate, bonus)[i // 2][:, 2 * (i % 2):2 * (i % 2) + 2, :] for i in range(4)]
        wg_raw = edge[3][0:E, 0, :]
        params_raw = edge[3][0:ROWS, 1, 0:P]
        b2_raw = edge[3][:, 2, :]
        b2_rest = edge[3][:, 3, :]
        b2_mid = den_state[:, 0, 0:128].bitcast(BF16)
        w1_raw = hidden[:, 0:2, :, :].rearrange("p a b c -> p a (b c)")
        halo_planes = v_sb[:, 0:3, :]
        halo_gray = v_sb[:, 3, :]
        halo_hi, halo_lo = [t[:, 0, :, :].rearrange("p i t -> p (i t)")[:, 0:D + 2]
                            for t in (normed2_hi, normed2_lo)]
        w1_scaled = resid[0][:, :, :].rearrange("p (a b) d -> p a (b d)", a=CH)
        shift = normed2[:, 0:3, 0:P]
        band = normed[:, 0:3, :].rearrange("p a (b m) -> p (a b) m", b=2)

        bank = [ctx.enter_context(nc.psum_tensor(f"bank{i}", [P, 512], F32)) for i in range(8)]
        logits_parts = bank[7][:, 0:NB * 2 * E].rearrange("p (b e) -> p b e", b=NB)
        route_ps = bank[2][:, 0:256].bitcast(BF16)
        BANK_EDGE, BANK_WO, BANK_K, BANK_V, BANK_R = (0, 1, 2, 3), (4, 5), (6, 7), (0, 1), (7, 0)
        BANK_W = (5, 6, 7, 4)
        BANK_HIDDEN, BANK_NORMED2, BANK_Y, BANK_NORMED = (3, 4, 5, 6), (1, 2), (3, 4), (5, 6)

        params_ps, wg_ps, b1_ps = bank[0][:, 0:ROWS], bank[5][:, 0:CH * E], bank[5][:, 64:64 + NM * E]

        planes_in = [sem(f"planes_in{i}") for i in range(2)]
        s_params_in, s_scharr_in, s_scharr_dj_in = sem("params_in"), sem("scharr_in"), sem("scharr_dj_in")
        s_wo_in = sem("wo_in")
        s_w_in, s_wg_in, s_w1_in, s_w2_in = sem("w_in"), sem("wg_in"), sem("w1_in"), sem("w2_in")
        s_b2_in, s_halo_planes_in = sem("b2_in"), sem("halo_planes_in")
        s_cleared, s_built = sem("cleared"), sem("built")
        s_dve_setup, s_act_setup, s_pe_setup = sem("dve_setup"), sem("act_setup"), sem("pe_setup")

        halo_in = sem("halo_in")
        stored = [sem(f"stored{i}") for i in range(4)]
        s_red, s_red_green, s_gray, s_gray_hi, s_gray_lo = [sem(n) for n in (
            "red", "red_green", "gray_done", "gray_hi_done", "gray_lo_done")]
        s_edge_ps, s_abs, s_edge = sem("edge_ps"), sem("abs"), sem("edge_done")
        s_stats, s_moments, s_log_var, s_rstd = [[sem(f"{n}{i}") for i in range(2)] for n in (
            "stats", "moments", "log_var", "rstd")]
        s_normed, s_normed_ps, s_normed_t = sem("normed"), sem("normed_ps"), sem("normed_t")
        s_diff, s_mixed, s_proj_ps = sem("diff"), sem("mixed"), sem("proj_ps")
        s_mixed_hi, s_mixed_lo = sem("mixed_hi_done"), sem("mixed_lo_done")
        s_rwkv_hi, s_rwkv_lo = sem("rwkv_hi_done"), sem("rwkv_lo_done")
        s_v, s_gate = sem("v"), sem("gate")
        s_max, s_gap, s_fresh_arg, s_decay_arg, s_cap_arg, s_exps = [sem(n) for n in (
            "max_done", "gap_done", "fresh_arg", "decay_arg", "cap_arg", "exps")]
        s_den_state, s_den, s_fresh_v, s_num_state = [sem(n) for n in (
            "den_state_done", "den_done", "fresh_v_done", "num_state_done")]
        s_log_den, s_recip, s_bonus_v, s_num, s_gated, s_rwkv = [sem(n) for n in (
            "log_den", "recip", "bonus_v", "num", "gated", "rwkv_done")]
        s_wo_ps, s_resid = sem("wo_ps"), sem("resid_done")
        s_normed2, s_normed2_ps, s_normed2_hi, s_normed2_lo = [sem(n) for n in (
            "normed2_done", "normed2_ps", "normed2_hi_done", "normed2_lo_done")]
        s_shift = sem("shift")
        s_normed_i = (s_normed, s_normed2)
        s_logits_sum = sem("logits_sum")
        s_logits, s_best, s_hits, s_ranked, s_best_rank, s_route, s_route_ps, s_route_t = [sem(n) for n in (
            "logits", "best_done", "hits", "ranked", "best_rank_done", "route", "route_ps", "route_t")]
        s_hidden_ps, s_hidden, s_y_ps, s_result = [sem(n) for n in (
            "hidden_ps", "hidden_done", "y_ps", "result_done")]

        def run_steps(eng, step, setup_before={}):
            for i in range(UNROLL):
                if i in setup_before:
                    setup_before[i]()
                step(Step(0, i, PAIRS))
            if UNROLL in setup_before:
                setup_before[UNROLL]()
            with eng.Fori(1, PAIRS // UNROLL) as j:
                for i in range(UNROLL):
                    step(Step(j, i, PAIRS))
            for i in range(UNROLL):
                step(Step(PAIRS // UNROLL, i, PAIRS))

        block = ctx.enter_context(nc.Block())

        @block.sync
        def _(sp):
            def load_planes(j, c, buf):
                for half in range(HALF):
                    first = j * (UNROLL * 6) + 6 * c
                    src = x_planes[bass.ds(first, 6), half * P:(half + 1) * P, :]
                    sp.dma_start(planes[buf][:, 2 * half:2 * half + 2, :, :].rearrange("p i c w -> p (i c) w"),
                                 src.rearrange("n p w -> p n w")).then_inc(planes_in[buf], 16)

            for i in range(3):
                sp.dma_start(halo_planes[:, i, :], x[:, i, P - 1:P + 1, :].rearrange("n r w -> n r w")
                             ).then_inc(s_halo_planes_in, 16)
            sp.dma_start(scharr_all[:, :], scharr.rearrange("o i h w -> (o i h w)")
                         .partition_broadcast(P)).then_inc(s_scharr_in, 16)
            for i in range(3):
                sp.dma_start(scharr_dj[32 * i:32 * i + 3, :], scharr.rearrange("o i h w -> w (o i h)"),
                             allow_slow_non_contiguous=True).then_inc(s_scharr_dj_in, 16)
            rows = [(ROW_W, w.rearrange("(r c) -> r c", c=P)), (ROW_U, u.rearrange("(r c) -> r c", c=P))]
            rows += [(r, t.rearrange("a b (r c) -> (a b r) c", c=P))
                     for r, t in zip(ROW_TM, (time_mix_k, time_mix_v, time_mix_r))]
            rows += [(ROW_SCALE, ln_scale.rearrange("e (r c) -> (e r) c", c=P)),
                     (ROW_BIAS, ln_bias.rearrange("e (r c) -> (e r) c", c=P)),
                     (ROW_B1, b1.rearrange("e h -> (e h)").rearrange("(r c) -> r c", c=P))]
            sp.wait_ge(s_cleared, CLEARED_B2)
            for r, src in rows:
                sp.dma_start(params_raw[r:r + src.shape[0], :], src).then_inc(s_params_in, 16)
            load_planes(0, 0, 0)
            for src, dst in zip((Wk, Wv, Wr), w_raw):
                sp.dma_start(dst, src.rearrange("(a p) c -> p a c", p=P)).then_inc(s_w_in, 16)

            def load_later_weights():
                for ct in range(CH):
                    sp.dma_start(w1_raw[:, ct, :].rearrange("p (e h) -> p e h", e=E),
                                 W1[:, ct * P:(ct + 1) * P, :].rearrange("e p h -> p e h")).then_inc(s_w1_in, 16)
                for i in range(3):
                    sp.dma_start(b2_raw[32 * i:32 * i + E, :], b2).then_inc(s_b2_in, 16)
                sp.dma_start(w_raw[3], Wo.rearrange("(a p) c -> p a c", p=P)).then_inc(s_wo_in, 16)
                sp.dma_start(wg_raw, Wg).then_inc(s_wg_in, 16)
                sp.dma_start(w2_sb[:, :, :], W2.rearrange("e h d -> (e h) d").rearrange("(m p) d -> p m d", p=P)
                             ).then_inc(s_w2_in, 16)

            sp.wait_ge(s_cleared, CLEARED_SHIFT)
            sp.wait_ge(s_dve_setup, SETUP_HALO)
            for i in range(4):
                part, rows = i // 2, slice(64 * (i % 2), 64 * (i % 2) + 64)
                sp.dma_start(gray_halo_dram[part, rows, :], (halo_hi, halo_lo)[part][rows, :].bitcast(F32)
                             ).then_inc(stored[i], 16)
            for i in range(4):
                sp.wait_ge(stored[i], 16)
            sp.wait_ge(s_built, 1)

            def step(at):
                if at.has(GRAY):
                    b = at.buf(GRAY)
                    sp.wait_ge(s_gray, at.count(GRAY, 1, 1, back=2))
                    if not at.first():
                        load_planes(at.j, at.u, b)
                    sp.wait_ge(s_edge_ps, at.count(GRAY, 4, 4, back=1))
                    for i, part in enumerate((0, 0, 1)):
                        row = at.j * (UNROLL * 4) + 4 * at.u
                        src = bass.AP(gray_halo_dram.tensor, part * P * (D + 2) + row * (D + 2),
                                      [[1, 3], [D + 2, 4], [1, D]])
                        dst = halo[32 * i:32 * i + 3, :, :, :].bitcast(F32).rearrange("p i r w -> p (i r) w")
                        sp.dma_start(dst, src).then_inc(halo_in, 16)
                if at.has(FFN):
                    b = at.buf(FFN, 4)
                    for half in range(HALF):
                        sp.wait_ge(s_result, at.results(half + 1))
                        first = at.j * (UNROLL * 2) + 2 * (at.u - FFN)
                        dst = out[bass.ds(first, 2), half * P:(half + 1) * P, :].rearrange("n p w -> p n w")
                        sp.dma_start(dst, edge[b][:, 2 * half:2 * half + 2, :]).then_inc(stored[b], 16)

            run_steps(sp, step, {1: load_later_weights})
            for i in range(4):
                sp.wait_ge(stored[i], 16 + 16 * HALF * PAIRS // 4)

        @block.gpsimd
        def _(pool):
            pool.memset(b2_raw, 0.0).then_inc(s_cleared, 1)
            for t in (halo_hi, halo_lo):
                pool.memset(t[:, 0:1].bitcast(F32), 0.0)
                pool.memset(t[:, D + 1:D + 2].bitcast(F32), 0.0)
            pool.memset(shift, 0.0).then_inc(s_cleared, 1)
            pool.wait_ge(s_cleared, CLEARED_SHIFT)
            for di in range(3):
                pool.affine_select(out=shift[:, di, :], in_=shift[:, di, :], compare_op=ALU.not_equal, fill=1.0,
                                   base=1 - di, pattern=[[-1, P]], channel_multiplier=1).then_inc(s_cleared, 1)
            pool.memset(mask_rows[:, :], MASK_OUT).then_inc(s_cleared, 1)
            pool.wait_ge(s_cleared, 6)
            pool.affine_select(out=mask_rows[:, :], in_=mask_rows[:, :], compare_op=ALU.is_ge, fill=0.0,
                               base=96 * H, pattern=[[1, E * H]], channel_multiplier=-H).then_inc(s_cleared, 1)
            pool.wait_ge(s_cleared, 7)
            pool.affine_select(out=mask_rows[:, :], in_=mask_rows[:, :], compare_op=ALU.is_ge, fill=0.0,
                               base=H - 1 - 96 * H, pattern=[[-1, E * H]], channel_multiplier=H).then_inc(s_cleared, 1)
            pool.memset(halo[:, :, :, :].bitcast(F32), 0.0)
            for g in (gray_hi, gray_lo):
                pool.memset(g[:, :, 0:1].bitcast(F32), 0.0)
                pool.memset(g[:, :, D + 1:D + 2].bitcast(F32), 0.0)
            pool.memset(normed_t[:, :, 0:1], 0.0)
            pool.memset(max_state[:, :, 0:1], NEVER)
            for t in (fresh, decay):
                pool.memset(t[:, :, 0:1], 0.0)
            for e in range(E):
                pool.memset(descending[:, e:e + 1], float(E - e))
            pool.memset(cap[:, :], BONUS_CAP)
            pool.memset(eps[:, 0:1], LN_EPS)
            pool.memset(eps[:, 1:2], LN_EPS * LN_EPS)
            pool.memset(band_halo[:, :, :].bitcast(F32), 0.0)
            pool.memset(b2_parts[:, :], 0.0)
            pool.memset(route[:, :, :], 0.0).then_inc(s_built, 1)

        @block.vector
        def _(dve):
            own = [0]

            def done(ins):
                own[0] += 1
                ins.then_inc(s_dve_setup, 1)
                dve.wait_ge(s_dve_setup, own[0])

            dve.wait_ge(s_halo_planes_in, 48)
            done(dve.tensor_scalar(halo_gray, halo_planes[:, 0, :], GRAY_WEIGHTS[0], None, ALU.mult))
            for i in (1, 2):
                done(dve.scalar_tensor_tensor(out=halo_gray, in0=halo_planes[:, i, :], scalar=GRAY_WEIGHTS[i],
                                              in1=halo_gray, op0=ALU.mult, op1=ALU.add))
            dve.wait_ge(s_act_setup, 1)
            done(dve.tensor_tensor(halo_lo[:, 1:D + 1], halo_gray, halo_hi[:, 1:D + 1].bitcast(F32), ALU.subtract))

            dve.wait_ge(s_scharr_in, 16)
            dve.wait_ge(s_scharr_dj_in, 48)
            dve.wait_ge(s_cleared, CLEARED_BUILT_SHIFT)
            done(dve.tensor_scalar(scharr_all[:, :], scharr_all[:, :], 0.5, None, ALU.mult))
            for i in range(3):
                rows = slice(32 * i, 32 * i + 3)
                dve.tensor_scalar(scharr_dj[rows, :], scharr_dj[rows, :], 0.5, None, ALU.mult)
            done(dve.tensor_copy(ident[:, :], shift[:, 1, :]))
            for i in range(3):
                rows = slice(32 * i, 32 * i + 3)
                dve.tensor_copy(scharr_hi[rows, :], scharr_dj[rows, :])
            done(dve.tensor_copy(ident_bf[:, :], ident[:, :]))
            for i in range(3):
                rows = slice(32 * i, 32 * i + 3)
                dve.tensor_tensor(scharr_lo[rows, :], scharr_dj[rows, :], scharr_hi[rows, :].bitcast(F32),
                                  ALU.subtract)
            for di in range(3):
                for c in range(2):
                    for dj in range(3):
                        weight = scharr_all[:, 9 * c + 3 * di + dj:9 * c + 3 * di + dj + 1]
                        b = band[:, 3 * c + dj, :]
                        if di == 0:
                            ins = dve.tensor_scalar(b, shift[:, di, :], weight, None, ALU.mult)
                        else:
                            ins = dve.scalar_tensor_tensor(out=b, in0=shift[:, di, :], scalar=weight, in1=b,
                                                           op0=ALU.mult, op1=ALU.add)
                done(ins)
            done(dve.tensor_copy(band_hi[:, :, :], band))
            done(dve.tensor_tensor(band_lo[:, :, :], band, band_hi[:, :, :].bitcast(F32), ALU.subtract))
            dve.wait_ge(s_built, 1)
            for half, (col, di) in enumerate(((P - 1, 2), (0, 0))):
                for c in range(2):
                    for i, part in enumerate((scharr_hi, scharr_lo, scharr_hi)):
                        rows = slice(32 * i, 32 * i + 3)
                        ins = dve.tensor_copy(band_halo[rows, 2 * half + c, col:col + 1],
                                              part[rows, 3 * c + di:3 * c + di + 1].bitcast(F32))
            done(ins)
            dve.wait_ge(s_pe_setup, 1)
            done(dve.tensor_copy(params[:, :], params_ps))
            assert own[0] == SETUP_CONV

            def setup_projections():
                dve.tensor_copy(best[:, 0:1], cap[:, :]).then_inc(s_result, RESULTS_AHEAD)
                dve.tensor_scalar(cap_less_u[:, :], params[:, ROW_U:ROW_U + CH], -1.0, BONUS_CAP,
                                  ALU.mult, ALU.add)
                dve.wait_ge(s_act_setup, 2)
                done(dve.tensor_scalar(neg_exp_w[:, :], exp_w[:, :], -1.0, None, ALU.mult))
                dve.wait_ge(s_pe_setup, 2)
                for i in range(3):
                    split_weights(i, 1.0)
                assert own[0] == SETUP_PROJECTIONS

            def setup_first():
                setup_projections()
                setup_experts()

            def split_weights(i, scale):
                hi, lo = [t[i][:, :, :].rearrange("p a d -> p (a d)") for t in (w_hi, w_lo)]
                done(dve.tensor_scalar(hi, bank[BANK_W[i]][:, :], scale, None, ALU.mult))
                done(dve.scalar_tensor_tensor(out=lo, in0=bank[BANK_W[i]][:, :], scalar=scale,
                                              in1=hi.bitcast(F32), op0=ALU.mult, op1=ALU.subtract))

            def setup_output_projection():
                dve.wait_ge(s_pe_setup, 3)
                split_weights(3, 0.5)
                wg_t = wg_ps.rearrange("p (c e) -> p c e", c=CH)
                done(dve.tensor_copy(wg_parts[:, :, 0:E], wg_t))
                dve.tensor_tensor(wg_parts[:, :, E:2 * E], wg_t, wg_parts[:, :, 0:E].bitcast(F32), ALU.subtract)
                for m in range(NM):
                    for i in range(2):
                        rows = slice(64 * i, 64 * i + 64)
                        col = m * E + 2 * m + i
                        ins = dve.tensor_tensor(b1_full[rows, m:m + 1], b1_ps[rows, col:col + 1],
                                                params[rows, ROW_B1 + m:ROW_B1 + m + 1], ALU.add)
                done(ins)
                assert own[0] == SETUP_ALL

            def setup_experts():
                dve.wait_ge(s_w1_in, 32)
                for ct in range(CH):
                    cols = params[:, ROW_SCALE + ct:ROW_BIAS:CH]
                    done(dve.tensor_tensor(w1_scaled[:, ct, :].rearrange("p (e h) -> p e h", e=E),
                                           w1_raw[:, ct, :].rearrange("p (e h) -> p e h", e=E),
                                           cols.unsqueeze(2).to_broadcast([P, E, H]), ALU.mult))
                done(dve.tensor_copy(w1_hi[:, :, :], w1_scaled))
                done(dve.tensor_tensor(w1_lo[:, :, :], w1_scaled, w1_hi[:, :, :].bitcast(F32), ALU.subtract))
                dve.wait_ge(s_b2_in, 48)
                b2_high = b2_parts[:, :]
                done(dve.tensor_copy(b2_mid, b2_raw))
                done(dve.tensor_tensor(b2_rest, b2_raw, b2_mid, ALU.subtract))
                done(dve.tensor_copy(b2_high[0:E, :], b2_mid[0:E, :]))
                done(dve.tensor_copy(b2_mid, b2_rest))
                done(dve.tensor_copy(b2_high[32:32 + E, :], b2_mid[32:32 + E, :]))
                done(dve.tensor_tensor(b2_rest, b2_rest, b2_mid, ALU.subtract))
                done(dve.tensor_copy(b2_high[64:64 + E, :], b2_rest[64:64 + E, :]))
                assert own[0] == SETUP_EXPERTS

            def layer_norm_moments(i, src):
                for b in range(NB):
                    ins = dve.bn_stats(stats[i][:, b, :], src[:, b, :])
                ins.then_inc(s_stats[i], 1)

            def aggregate(i):
                for b in range(NB):
                    ins = dve.bn_aggr(moments[i][:, b, :], stats[i][:, b, :])
                ins.then_inc(s_moments[i], 1)

            def residual(half, at):
                dve.wait_ge(s_wo_ps, at.count(PROJ, 2, half + 1))
                dve.tensor_tensor(resid[at.buf(PROJ)][:, 2 * half:2 * half + 2, :], pair_view(bank[BANK_WO[half]]),
                                  edge[at.buf(PROJ, 4)][:, 2 * half:2 * half + 2, :], ALU.add
                                  ).then_inc(s_resid, 1)

            def gray_and_blue(at):
                dve.wait_ge(s_red_green, at.count(GRAY, 1, 1))
                dve.scalar_tensor_tensor(out=gray[:, :, :], in0=planes[at.buf(GRAY)][:, :, 2, :],
                                         scalar=GRAY_WEIGHTS[2], in1=gray[:, :, :],
                                         op0=ALU.mult, op1=ALU.add).then_inc(s_gray, 1)

            def gray_rest(at):
                dve.wait_ge(s_gray_hi, at.count(GRAY, 1, 1))
                dve.tensor_tensor(gray_lo[:, :, 1:D + 1], gray[:, :, :], gray_hi[:, :, 1:D + 1].bitcast(F32),
                                  ALU.subtract).then_inc(s_gray_lo, 1)

            def edge_sum(half, at):
                dve.wait_ge(s_abs, at.count(EDGE, 4, 2 * half + 2))
                hh = edge[at.buf(EDGE, 4)][:, 2 * half:2 * half + 2, :].rearrange("p i w -> p (i w)")
                dve.tensor_tensor(hh, hh, abs_a[:, half, :], ALU.add).then_inc(s_edge, 1)

            def step(at):
                if at.has(FFN):
                    dve.wait_ge(s_logits, at.count(FFN, 1, 1))
                    dve.tensor_reduce(logits[:, :, :], logits_parts.rearrange("p b (n e) -> p b e n", n=2),
                                      AXIS_X, ALU.add).then_inc(s_logits_sum, 1)
                if at.has(EDGE):
                    edge_sum(0, at)
                if at.has(WKV):
                    dve.wait_ge(s_gated, at.count(WKV, 1, 1, back=1))
                    mix(2, at)
                if at.has(EDGE):
                    edge_sum(1, at)
                if at.has(WKV):
                    dve.wait_ge(s_gap, at.count(WKV, 2, 2, back=1))
                    for ct in range(CH):
                        dve.wait_ge(s_proj_ps, at.count(WKV, 6, 1 + ct))
                        for i in range(2):
                            ins = dve.tensor_tensor_scan(
                                max_state[:, 2 * ct + i, 1:T + 1], neg_exp_w[:, ct:ct + 1].to_broadcast([P, T]),
                                bank[BANK_K[ct]][:, i * T:(i + 1) * T], NEVER, ALU.add, ALU.max)
                        ins.then_inc(s_max, 1)
                    dve.wait_ge(s_mixed_lo, at.count(WKV, 3, 1))
                    for ct in range(CH):
                        dve.wait_ge(s_max, at.count(WKV, 2, 1 + ct))
                        dve.tensor_tensor(gap[:, 2 * ct:2 * ct + 2, :], pair_view(bank[BANK_K[ct]]),
                                          max_state[:, 2 * ct:2 * ct + 2, 0:T], ALU.subtract).then_inc(s_gap, 1)
                if at.has(EDGE):
                    dve.wait_ge(s_edge, at.count(EDGE, 2, 2))
                    layer_norm_moments(0, edge[at.buf(EDGE, 4)])
                if at.has(FFN):
                    dve.wait_ge(s_logits_sum, at.count(FFN, 1, 1))
                    dve.tensor_reduce(best[:, :], logits[:, :, :], AXIS_X, ALU.max).then_inc(s_best, 1)
                    dve.wait_ge(s_best, at.count(FFN, 1, 1))
                    dve.tensor_tensor(rank[:, :, :], logits[:, :, :],
                                      best[:, :].unsqueeze(2).to_broadcast([P, NB, E]),
                                      ALU.is_equal).then_inc(s_hits, 1)
                    dve.wait_ge(s_hits, at.count(FFN, 1, 1))
                    dve.tensor_tensor(rank[:, :, :], rank[:, :, :],
                                      descending[:, :].unsqueeze(1).to_broadcast([P, NB, E]), ALU.mult
                                      ).then_inc(s_ranked, 1)
                    dve.wait_ge(s_ranked, at.count(FFN, 1, 1))
                    dve.tensor_reduce(best_rank[:, :], rank[:, :, :], AXIS_X, ALU.max).then_inc(s_best_rank, 1)
                    dve.wait_ge(s_best_rank, at.count(FFN, 1, 1))
                    groups = route[:, :, :].rearrange("p b (g e) -> p b g e", g=4)
                    dve.tensor_tensor(groups[:, :, 0:3, 0:E], rank[:, :, :].unsqueeze(2).to_broadcast([P, NB, 3, E]),
                                      best_rank[:, :].unsqueeze(2).unsqueeze(3).to_broadcast([P, NB, 3, E]),
                                      ALU.is_equal)
                    dve.tensor_tensor(groups[:, :, 3, 0:E], rank[:, :, :],
                                      best_rank[:, :].unsqueeze(2).to_broadcast([P, NB, E]),
                                      ALU.not_equal).then_inc(s_route, 1)
                if at.has(PROJ):
                    dve.wait_ge(s_result, at.results(2, back=1))
                    residual(0, at)
                    residual(1, at)
                if at.has(PROJ):
                    dve.wait_ge(s_resid, at.count(PROJ, 2, 2))
                    layer_norm_moments(1, resid[at.buf(PROJ)])
                    dve.wait_ge(s_stats[1], at.count(PROJ, 1, 1))
                if at.has(EDGE):
                    dve.wait_ge(s_stats[0], at.count(EDGE, 1, 1))
                if at.has(GRAY):
                    b = at.buf(GRAY)
                    dve.wait_ge(s_red, at.count(GRAY, 1, 1))
                    dve.scalar_tensor_tensor(out=gray[:, :, :], in0=planes[b][:, :, 1, :], scalar=GRAY_WEIGHTS[1],
                                             in1=gray[:, :, :], op0=ALU.mult, op1=ALU.add).then_inc(s_red_green, 1)
                if at.has(EDGE):
                    aggregate(0)
                if at.has(PROJ):
                    aggregate(1)
                if at.has(WKV):
                    mixed_rest(2, WKV, at)
                if at.has(GRAY) and at.filling():
                    gray_and_blue(at)
                if at.has(EDGE):
                    dve.wait_ge(s_normed, at.count(EDGE, 1, 1, back=1))
                    dve.wait_ge(s_rstd[0], at.count(EDGE, 1, 1))
                    dve.scalar_tensor_tensor(out=neg_shift[:, :], in0=moments[0][:, :, 0], scalar=-1.0,
                                             in1=rstd[0][:, :], op0=ALU.mult, op1=ALU.mult).then_inc(s_shift, 1)
                if at.has(PROJ):
                    dve.wait_ge(s_rstd[1], at.count(PROJ, 1, 1))
                    dve.wait_ge(s_normed2_ps, at.count(PROJ, 2, 2, back=1))
                    for b in range(NB):
                        ins = dve.tensor_scalar(normed2[:, b, :], resid[at.buf(PROJ)][:, b, :],
                                                moments[1][:, b, 0:1], rstd[1][:, b:b + 1], ALU.subtract, ALU.mult)
                    ins.then_inc(s_normed2, 1)
                if at.has(GRAY) and not at.filling():
                    gray_and_blue(at)
                if at.has(WKV):
                    dve.wait_ge(s_exps, at.count(WKV, 3, 2))
                    dve.tensor_tensor_scan(flat(den_state), flat(decay), flat(fresh), 0.0,
                                           ALU.mult, ALU.add).then_inc(s_den_state, 1)
                    dve.wait_ge(s_v, at.count(WKV, 2, 2))
                    dve.wait_ge(s_den_state, at.count(WKV, 1, 1))
                    dve.tensor_tensor(fresh[:, :, 1:T + 1], fresh[:, :, 1:T + 1], v_sb[:, :, :],
                                      ALU.mult).then_inc(s_fresh_v, 1)
                    dve.wait_ge(s_exps, at.count(WKV, 3, 3))
                    dve.tensor_tensor(den[:, :, :], bonus[:, :, :], den_state[:, :, 0:T],
                                      ALU.add).then_inc(s_den, 1)
                    dve.tensor_tensor(bonus[:, :, :], bonus[:, :, :], v_sb[:, :, :], ALU.mult
                                      ).then_inc(s_bonus_v, 1)
                if at.has(GRAY) and at.filling():
                    gray_rest(at)
                if at.has(WKV):
                    dve.wait_ge(s_fresh_v, at.count(WKV, 1, 1))
                    dve.tensor_tensor_scan(flat(num_state), flat(decay), flat(fresh), 0.0,
                                           ALU.mult, ALU.add).then_inc(s_num_state, 1)
                    dve.wait_ge(s_num_state, at.count(WKV, 1, 1))
                    dve.wait_ge(s_bonus_v, at.count(WKV, 1, 1))
                    dve.tensor_tensor(bonus[:, :, :], bonus[:, :, :], num_state[:, :, 0:T], ALU.add
                                      ).then_inc(s_num, 1)
                if at.has(PROJ):
                    dve.wait_ge(s_hidden_ps, at.count(FFN, 4, 4))
                    for ct in range(CH):
                        dve.wait_ge(s_normed2_hi, at.count(PROJ, 2, ct + 1))
                        dve.tensor_tensor(normed2_lo[:, ct, :, :], pair_view(bank[BANK_NORMED2[ct]]),
                                          normed2_hi[:, ct, :, :].bitcast(F32), ALU.subtract
                                          ).then_inc(s_normed2_lo, 1)
                if at.has(WKV):
                    dve.wait_ge(s_num, at.count(WKV, 1, 1))
                    dve.wait_ge(s_gate, at.count(WKV, 2, 2))
                    dve.scalar_tensor_tensor(out=bonus[:, :, :], in0=gate[:, :, :], scalar=1.0, in1=bonus[:, :, :],
                                             op0=ALU.add, op1=ALU.mult).then_inc(s_gated, 1)
                if at.has(GRAY) and not at.filling():
                    gray_rest(at)
                if at.has(FFN):
                    dve.wait_ge(s_resid, at.count(FFN, 2, 2))
                    for half in range(HALF):
                        dve.wait_ge(s_y_ps, at.count(FFN, 2, half + 1))
                        dve.tensor_tensor(edge[at.buf(FFN, 4)][:, 2 * half:2 * half + 2, :],
                                          pair_view(bank[BANK_Y[half]]), resid[at.buf(FFN)][:, 2 * half:2 * half + 2, :],
                                          ALU.add).then_inc(s_result, 1)
                if at.has(WKV):
                    dve.wait_ge(s_gated, at.count(WKV, 1, 1))
                    dve.wait_ge(s_recip, at.count(WKV, 1, 1))
                    dve.tensor_tensor(rwkv, bonus[:, :, :], den[:, :, :], ALU.mult).then_inc(s_rwkv, 1)
                if at.has(EDGE):
                    dve.wait_ge(s_normed_t, at.count(EDGE, 2, 2))
                    dve.tensor_tensor(step_diff[:, :, :], normed_t[:, :, 1:T + 1], normed_t[:, :, 0:T],
                                      ALU.subtract).then_inc(s_diff, 1)
                if at.has(WKV):
                    dve.wait_ge(s_rwkv_hi, at.count(WKV, 1, 1))
                    dve.wait_ge(s_wo_ps, at.count(PROJ, 2, 2))
                    dve.tensor_tensor(rwkv_lo[:, :, :], rwkv, rwkv_hi[:, :, :].bitcast(F32), ALU.subtract
                                      ).then_inc(s_rwkv_lo, 1)
                if at.has(EDGE):
                    dve.wait_ge(s_diff, at.count(EDGE, 1, 1))
                    dve.wait_ge(s_cap_arg, at.count(WKV, 1, 1))
                    mix(0, at)
                    dve.wait_ge(s_bonus_v, at.count(WKV, 1, 1))
                    mix(1, at)
                    mixed_rest(0, EDGE, at)
                    mixed_rest(1, EDGE, at)

            def mix(i, at):
                for ct in range(CH):
                    seg = slice(2 * ct, 2 * ct + 2)
                    ins = dve.scalar_tensor_tensor(
                        out=mixed[i][:, seg, :], in0=step_diff[:, seg, :],
                        scalar=params[:, ROW_TM[i] + ct:ROW_TM[i] + ct + 1],
                        in1=normed_t[:, seg, 0:T], op0=ALU.mult, op1=ALU.add)
                ins.then_inc(s_mixed, 1)

            def mixed_rest(i, stage, at):
                dve.wait_ge(s_mixed_hi, at.count(stage, 3, i + 1))
                dve.wait_ge(s_proj_ps, at.count(stage, 6, 2 * i + 2, back=1))
                dve.tensor_tensor(mixed_lo[i][:, :, :], mixed[i], mixed_hi[i][:, :, :].bitcast(F32), ALU.subtract
                                  ).then_inc(s_mixed_lo, 1)

            def flat(t):
                return t[:, :, :].rearrange("p s t -> p (s t)")

            def pair_view(ps):
                return ps[:, :].rearrange("p (i w) -> p i w", i=2)

            run_steps(dve, step, {1: setup_first, 2: setup_output_projection})

        @block.scalar
        def _(act):
            act.wait_ge(s_dve_setup, SETUP_HALO_GRAY)
            act.activation(halo_hi[:, 1:D + 1], halo_gray, ACT.Copy).then_inc(s_act_setup, 1)
            act.wait_ge(s_dve_setup, SETUP_PARAMS)
            act.activation(exp_w[:, :], params[:, ROW_W:ROW_W + CH], ACT.Exp).then_inc(s_act_setup, 1)

            def reciprocal_std(i, stage, at):
                act.wait_ge(s_moments[i], at.count(stage, 1, 1))
                act.activation(log_var[i][:, :], moments[i][:, :, 1], ACT.Ln, bias=eps[:, i:i + 1],
                               scale=1.0 if i == 0 else 1.0 + LN_EPS).then_inc(s_log_var[i], 1)
                act.wait_ge(s_log_var[i], at.count(stage, 1, 1))
                act.activation(rstd[i][:, :], log_var[i][:, :], ACT.Exp, scale=-0.5).then_inc(s_rstd[i], 1)

            def absolute(half, at):
                b = at.buf(EDGE, 4)
                act.wait_ge(s_rwkv, at.count(PROJ, 1, 1))
                act.wait_ge(stored[b], 16 + at.dma_count(FFN, 2, n=4, back=1))
                for c, dst in enumerate((abs_a[:, half, :], edge[b][:, 2 * half:2 * half + 2, :]
                                         .rearrange("p i w -> p (i w)"))):
                    act.wait_ge(s_edge_ps, at.count(EDGE, 4, 2 * half + c + 1))
                    act.activation(dst, bank[BANK_EDGE[2 * half + c]][:, :], ACT.Abs).then_inc(s_abs, 1)

            def step(at):
                if at.has(EDGE):
                    absolute(0, at)
                if at.has(GRAY):
                    b = at.buf(GRAY)
                    act.wait_ge(planes_in[b], at.dma_count(GRAY, 2))
                    act.wait_ge(s_gray_lo, at.count(GRAY, 1, 1, back=1))
                    act.activation(gray[:, :, :], planes[b][:, :, 0, :], ACT.Copy, scale=GRAY_WEIGHTS[0]
                                   ).then_inc(s_red, 1)
                if at.has(EDGE):
                    absolute(1, at)
                if at.has(WKV):
                    mixed_high(2, WKV, at)
                if at.u == 0:
                    act.preload_act_table_set("natural_log_exp_and_others")
                if at.has(WKV):
                    act.wait_ge(s_mixed_lo, at.count(WKV, 3, 2))
                    copy_v(0, at)
                    act.wait_ge(s_num_state, at.count(WKV, 1, 1, back=1))
                    for ct in range(CH):
                        seg = slice(2 * ct, 2 * ct + 2)
                        act.wait_ge(s_gap, at.count(WKV, 2, 1 + ct))
                        ins = act.activation(fresh[:, seg, 1:T + 1], gap[:, seg, :], ACT.Relu,
                                             bias=neg_exp_w[:, ct:ct + 1], scale=-1.0)
                    ins.then_inc(s_fresh_arg, 1)
                    for ct in range(CH):
                        seg = slice(2 * ct, 2 * ct + 2)
                        ins = act.activation(decay[:, seg, 1:T + 1], gap[:, seg, :], ACT.Relu,
                                             bias=exp_w[:, ct:ct + 1])
                    ins.then_inc(s_decay_arg, 1)
                    copy_v(1, at)
                if at.has(EDGE) and at.filling() and not at.has(PROJ):
                    reciprocal_std(0, EDGE, at)
                if at.has(WKV):
                    act.wait_ge(s_fresh_arg, at.count(WKV, 1, 1))
                    act.activation(fresh[:, :, 1:T + 1], fresh[:, :, 1:T + 1], ACT.Exp, scale=-1.0).then_inc(s_exps, 1)
                    act.wait_ge(s_decay_arg, at.count(WKV, 1, 1))
                    act.activation(decay[:, :, 1:T + 1], decay[:, :, 1:T + 1], ACT.Exp, scale=-1.0
                                   ).then_inc(s_exps, 1)
                if at.has(FFN):
                    act.wait_ge(s_route_ps, at.count(FFN, 1, 1))
                    act.activation(route_t[:, :, :].rearrange("p i t -> p (i t)"), route_ps, ACT.Copy
                                   ).then_inc(s_route_t, 1)
                if at.has(WKV):
                    act.wait_ge(s_rwkv_lo, at.count(WKV, 1, 1, back=1))
                    for ct in range(CH):
                        seg = slice(2 * ct, 2 * ct + 2)
                        ins = act.activation(bonus[:, seg, :], gap[:, seg, :], ACT.Relu,
                                             bias=cap_less_u[:, ct:ct + 1], scale=-1.0)
                    ins.then_inc(s_cap_arg, 1)
                    act.wait_ge(s_cap_arg, at.count(WKV, 1, 1))
                    act.activation(bonus[:, :, :], bonus[:, :, :], ACT.Exp, bias=cap[:, :], scale=-1.0
                                   ).then_inc(s_exps, 1)
                if at.has(EDGE) and (at.has(PROJ) or not at.filling()):
                    reciprocal_std(0, EDGE, at)
                if at.has(PROJ):
                    reciprocal_std(1, PROJ, at)
                if at.has(EDGE) and at.filling():
                    normalise(at)
                if at.has(GRAY) and at.filling():
                    gray_high(at)
                if at.has(FFN):
                    for m in range(NM):
                        act.wait_ge(s_hidden_ps, at.count(FFN, 4, m + 1))
                        act.activation(hidden[:, m, :, :], pair_view(bank[BANK_HIDDEN[m]]), ACT.Gelu,
                                       bias=b1_full[:, m:m + 1]).then_inc(s_hidden, 1)
                if at.has(WKV):
                    act.wait_ge(s_mixed_lo, at.count(WKV, 3, 3))
                    gate_of(0, at)
                if at.has(PROJ):
                    act.wait_ge(s_hidden_ps, at.count(FFN, 4, 4))
                    for ct in range(CH):
                        act.wait_ge(s_normed2_ps, at.count(PROJ, 2, ct + 1))
                        act.activation(normed2_hi[:, ct, :, :], pair_view(bank[BANK_NORMED2[ct]]), ACT.Copy
                                       ).then_inc(s_normed2_hi, 1)
                if at.has(WKV):
                    gate_of(1, at)
                if at.has(EDGE) and not at.filling():
                    normalise(at)
                if at.has(GRAY) and not at.filling():
                    gray_high(at)
                if at.has(WKV):
                    act.preload_act_table_set("natural_log_exp_and_others")
                    act.wait_ge(s_den, at.count(WKV, 1, 1))
                    act.activation(den[:, :, :], den[:, :, :], ACT.Ln).then_inc(s_log_den, 1)
                    act.wait_ge(s_log_den, at.count(WKV, 1, 1))
                    act.activation(den[:, :, :], den[:, :, :], ACT.Exp, scale=-1.0).then_inc(s_recip, 1)
                if at.has(EDGE):
                    act.wait_ge(s_mixed, at.count(EDGE, 3, 3, back=1))
                    for ct in range(CH):
                        act.wait_ge(s_normed_ps, at.count(EDGE, 2, ct + 1))
                        act.activation(normed_t[:, 2 * ct:2 * ct + 2, 1:T + 1], pair_view(bank[BANK_NORMED[ct]]),
                                       ACT.Copy).then_inc(s_normed_t, 1)
                if at.has(WKV):
                    act.wait_ge(s_wo_ps, at.count(PROJ, 2, 2))
                    act.wait_ge(s_rwkv, at.count(WKV, 1, 1))
                    act.activation(rwkv_hi[:, :, :], rwkv, ACT.Copy).then_inc(s_rwkv_hi, 1)
                if at.has(EDGE):
                    mixed_high(0, EDGE, at)
                    mixed_high(1, EDGE, at)

            def normalise(at):
                act.wait_ge(s_normed_ps, at.count(EDGE, 2, 2, back=1))
                act.wait_ge(s_mixed, at.count(EDGE, 3, 3, back=1))
                act.wait_ge(s_shift, at.count(EDGE, 1, 1))
                for b in range(NB):
                    ins = act.activation(normed[:, b, :], edge[at.buf(EDGE, 4)][:, b, :], ACT.Identity,
                                         bias=neg_shift[:, b:b + 1], scale=rstd[0][:, b:b + 1])
                ins.then_inc(s_normed, 1)

            def gray_high(at):
                act.wait_ge(s_gray, at.count(GRAY, 1, 1))
                act.wait_ge(s_edge_ps, at.count(GRAY, 4, 4, back=1))
                act.activation(gray_hi[:, :, 1:D + 1], gray[:, :, :], ACT.Copy).then_inc(s_gray_hi, 1)

            def mixed_high(i, stage, at):
                act.wait_ge(s_proj_ps, at.count(stage, 6, 2 * i + 2, back=1))
                act.wait_ge(s_mixed, at.count(stage, 3, i + 1))
                act.activation(mixed_hi[i][:, :, :], mixed[i], ACT.Copy).then_inc(s_mixed_hi, 1)

            def gate_of(ct, at):
                act.wait_ge(s_proj_ps, at.count(WKV, 6, 5 + ct))
                act.activation(gate[:, 2 * ct:2 * ct + 2, :], pair_view(bank[BANK_R[ct]]), ACT.Tanh, scale=0.5
                               ).then_inc(s_gate, 1)

            def copy_v(ct, at):
                act.wait_ge(s_proj_ps, at.count(WKV, 6, 3 + ct))
                act.activation(v_sb[:, 2 * ct:2 * ct + 2, :], pair_view(bank[BANK_V[ct]]), ACT.Copy
                               ).then_inc(s_v, 1)

            def pair_view(ps):
                return ps[:, :].rearrange("p (i w) -> p i w", i=2)

            act.wait_ge(s_dve_setup, SETUP_CONV)
            run_steps(act, step, {2: lambda: act.wait_ge(s_dve_setup, SETUP_PROJECTIONS)})

        @block.tensor
        def _(pe):
            def transposed_weights(i):
                for ct in range(CH):
                    for dt in range(CH):
                        ins = pe.transpose(bank[BANK_W[i]][:, ct * D + dt * P:ct * D + (dt + 1) * P],
                                           w_raw[i][:, dt, ct * P:(ct + 1) * P], ident[:, :])
                return ins

            pe.wait_ge(s_dve_setup, SETUP_IDENT)
            pe.wait_ge(s_params_in, 16 * 8)
            pe.transpose(params_ps, params_raw, ident[0:ROWS, 0:ROWS]).then_inc(s_pe_setup, 1)
            pe.wait_ge(s_w_in, 48)
            for i in range(3):
                ins = transposed_weights(i)
            ins.then_inc(s_pe_setup, 1)
            pe.wait_ge(s_dve_setup, SETUP_CONV)

            def before_projections():
                pe.wait_ge(s_dve_setup, SETUP_PROJECTIONS)
                pe.wait_ge(s_wo_in, 16)
                transposed_weights(3)
                pe.wait_ge(s_wg_in, 16)
                pe.wait_ge(s_normed_t, 1)
                for ct in range(CH):
                    pe.transpose(wg_ps[:, ct * E:(ct + 1) * E], wg_raw[:, ct * P:(ct + 1) * P], ident[0:E, 0:E])
                pe.wait_ge(s_w1_in, 32)
                for m in range(NM):
                    for ct in range(CH):
                        ins = pe.matmul(b1_ps[:, m * E:(m + 1) * E], w1_raw[:, ct, m * P:(m + 1) * P],
                                        params[:, ROW_BIAS + ct:ROW_B1:CH], start=(ct == 0), stop=(ct == CH - 1))
                ins.then_inc(s_pe_setup, 1)

            def before_experts():
                pe.wait_ge(s_w2_in, 16)
                pe.wait_ge(s_cleared, CLEARED_MASK)

            def project(at, i, ct, dst):
                for kt in range(CH):
                    for n, (weights, part) in enumerate(((w_hi, mixed_hi), (w_lo, mixed_hi), (w_hi, mixed_lo))):
                        ins = pe.matmul(dst[:, :], weights[i][:, kt, ct * P:(ct + 1) * P],
                                        part[i][:, 2 * kt:2 * kt + 2, :].rearrange("p i t -> p (i t)"),
                                        start=(kt == 0 and n == 0), stop=(kt == CH - 1 and n == 2))
                ins.then_inc(s_proj_ps, 1)

            def step(at):
                if at.has(EDGE):
                    pe.wait_ge(s_gray_lo, at.count(EDGE, 1, 1))
                    pe.wait_ge(halo_in, at.count(EDGE, 48, 48))
                    for n in range(2 * HALF):
                        half, c = divmod(n, 2)
                        if n == 0:
                            pe.wait_ge(s_gate, at.count(WKV, 2, 2, back=1))
                        elif n < 3:
                            pe.wait_ge(s_normed2_lo, at.count(PROJ, 2, n, back=1))
                        else:
                            pe.wait_ge(s_result, at.results(1, back=1))
                        ps = bank[BANK_EDGE[n]]
                        for dj in range(3):
                            for i, (weights, part) in enumerate(((band_hi, gray_hi), (band_lo, gray_hi),
                                                                 (band_hi, gray_lo))):
                                pe.matmul(ps[:, :], weights[:, 3 * c + dj, :],
                                          part[:, 2 * half:2 * half + 2, dj:dj + D],
                                          start=(dj == 0 and i == 0), stop=False)
                        pe.matmul(ps[:, :], band_halo[:, 2 * half + c, :], halo[:, :, 1 - half, :],
                                  start=False, stop=True).then_inc(s_edge_ps, 1)
                if at.has(WKV):
                    pe.wait_ge(s_mixed_lo, at.count(WKV, 3, 1))
                    pe.wait_ge(s_normed_t, at.count(WKV, 2, 2))
                    project(at, 0, 0, bank[BANK_K[0]])
                    pe.wait_ge(s_gate, at.count(WKV, 2, 1, back=1))
                    if at.has(FFN):
                        pe.wait_ge(s_logits_sum, at.count(FFN, 1, 1))
                    project(at, 0, 1, bank[BANK_K[1]])
                    pe.wait_ge(s_mixed_lo, at.count(WKV, 3, 2))
                    for ct in range(CH):
                        pe.wait_ge(s_abs, at.count(EDGE, 4, ct + 1))
                        project(at, 1, ct, bank[BANK_V[ct]])
                if at.has(PROJ):
                    pe.wait_ge(s_rwkv_lo, at.count(PROJ, 1, 1))
                    pe.wait_ge(s_result, at.results(2, back=1))
                    output_projection(0, at)
                    pe.wait_ge(s_normed_t, at.count(EDGE, 2, 1, back=1))
                    output_projection(1, at)
                if at.has(FFN):
                    pe.wait_ge(s_normed2_lo, at.count(FFN, 2, 2))
                    for m in range(NM):
                        ps = bank[BANK_HIDDEN[m]]
                        if m == 0:
                            pe.wait_ge(s_abs, at.count(EDGE, 4, 4))
                            pe.wait_ge(s_result, at.results(1, back=1))
                        elif m < 3:
                            pe.wait_ge(s_resid, at.count(PROJ, 2, m))
                        else:
                            pe.wait_ge(s_gap, at.count(WKV, 2, 1))
                        for kt in range(CH):
                            for n, (weights, part) in enumerate(((w1_hi, normed2_hi), (w1_lo, normed2_hi),
                                                                 (w1_hi, normed2_lo))):
                                pe.matmul(ps[:, :], weights[:, kt, m * P:(m + 1) * P],
                                          part[:, kt, :, :].rearrange("p i t -> p (i t)"),
                                          start=(kt == 0 and n == 0), stop=False)
                        if m == 0:
                            pe.wait_ge(s_route, at.count(FFN, 1, 1))
                            pe.wait_ge(s_abs, at.count(EDGE, 4, 3))
                            for i in range(2):
                                for half in range(HALF):
                                    col = i * T + half * P
                                    ins = pe.transpose(route_ps[:, col:col + P], route[:, 2 * half + i, :], ident_bf[:, :])
                            ins.then_inc(s_route_ps, 1)
                        if m == 1:
                            pe.wait_ge(s_route_t, at.count(FFN, 1, 1))
                        for n in ([], [0, 1], [2], [3])[m]:
                            pe.matmul(bank[BANK_HIDDEN[n]][:, :], mask_rows[:, n * P:(n + 1) * P],
                                      route_t[:, :, :].rearrange("p i t -> p (i t)"),
                                      start=False, stop=True).then_inc(s_hidden_ps, 1)
                if at.has(WKV):
                    pe.wait_ge(s_mixed_lo, at.count(WKV, 3, 3))
                    pe.wait_ge(s_gap, at.count(WKV, 2, 2))
                    project(at, 2, 0, bank[BANK_R[0]])
                if at.has(PROJ):
                    pe.wait_ge(s_normed2, at.count(PROJ, 1, 1))
                    pe.wait_ge(s_v, at.count(WKV, 2, 2))
                    transposed(normed2, BANK_NORMED2[0], 0).then_inc(s_normed2_ps, 1)
                    if at.has(FFN):
                        pe.wait_ge(s_route_t, at.count(FFN, 1, 1))
                    else:
                        pe.wait_ge(s_abs, at.count(EDGE, 4, 4))
                    transposed(normed2, BANK_NORMED2[1], 1).then_inc(s_normed2_ps, 1)
                if at.has(WKV):
                    pe.wait_ge(s_v, at.count(WKV, 2, 1))
                    project(at, 2, 1, bank[BANK_R[1]])
                if at.has(FFN):
                    pe.wait_ge(s_hidden, at.count(FFN, 4, 4))
                    for half in range(HALF):
                        for i in range(2):
                            ps = bank[BANK_Y[half]][:, i * D:(i + 1) * D]
                            rows = slice(half * P, (half + 1) * P)
                            for m in range(NM):
                                pe.matmul(ps, hidden[:, m, i, rows], w2_sb[:, m, :], start=(m == 0), stop=False)
                            ins = pe.matmul(ps, route_t[:, i, rows], b2_parts[:, :], start=False, stop=True)
                        ins.then_inc(s_y_ps, 1)
                if at.has(EDGE):
                    pe.wait_ge(s_normed, at.count(EDGE, 1, 1))
                    if not at.has(FFN):
                        pe.wait_ge(s_gap, at.count(WKV, 2, 1))
                        pe.wait_ge(s_resid, at.count(PROJ, 2, 2))
                    transposed(normed, BANK_NORMED[0], 0).then_inc(s_normed_ps, 1)
                    transposed(normed, BANK_NORMED[1], 1).then_inc(s_normed_ps, 1)
                if at.has(PROJ):
                    pe.wait_ge(s_normed2_lo, at.count(PROJ, 2, 2))
                    pe.wait_ge(s_gate, at.count(WKV, 2, 1))
                    for half in range(HALF):
                        for i in range(2):
                            rows = slice(half * P, (half + 1) * P)
                            for kt in range(CH):
                                for n, part in enumerate((normed2_hi, normed2_lo)):
                                    ins = pe.matmul(logits_parts[:, 2 * half + i, :], part[:, kt, i, rows],
                                                    wg_parts[:, kt, :],
                                                    start=(kt == 0 and n == 0), stop=(kt == CH - 1 and n == 1))
                    ins.then_inc(s_logits, 1)

            def transposed(src, n, ct):
                for i in range(2):
                    for half in range(HALF):
                        col = i * T + half * P
                        ins = pe.transpose(bank[n][:, col:col + P], src[:, 2 * half + i, ct * P:(ct + 1) * P],
                                           ident[:, :])
                return ins

            def output_projection(half, at):
                for i in range(2):
                    for kt in range(CH):
                        for n, (part, weights) in enumerate(((rwkv_hi, w_hi), (rwkv_hi, w_lo), (rwkv_lo, w_hi))):
                            ins = pe.matmul(bank[BANK_WO[half]][:, i * D:(i + 1) * D],
                                            part[:, 2 * kt + i, half * P:(half + 1) * P], weights[3][:, kt, :],
                                            start=(kt == 0 and n == 0), stop=(kt == CH - 1 and n == 2))
                ins.then_inc(s_wo_ps, 1)

            run_steps(pe, step, {2: before_projections, 3: lambda: pe.wait_ge(s_dve_setup, SETUP_ALL),
                                 UNROLL: before_experts})


_INS = ['x', 'L0_tok_scharr', 'L0_attn_w', 'L0_attn_u', 'L0_attn_time_mix_k', 'L0_attn_time_mix_v',
        'L0_attn_time_mix_r', 'L0_attn_Wk', 'L0_attn_Wv', 'L0_attn_Wr', 'L0_attn_Wo', 'L0_ffn_Wg',
        'L0_ffn_ln_scale', 'L0_ffn_ln_bias', 'L0_ffn_W1', 'L0_ffn_b1', 'L0_ffn_W2', 'L0_ffn_b2']
_OUTS = [((64, 256, 256), 'float32')]


def kernel(**inputs):
    import numpy as _np
    import concourse.bacc as _bacc
    from concourse import mybir as _mybir
    from concourse.bass_utils import run_bass_kernel_spmd as _run

    nc = _bacc.Bacc("TRN2", target_bir_lowering=False, num_devices=1)
    arrays, args = {}, []
    for name in _INS:
        a = _np.ascontiguousarray(inputs[name])
        arrays[f"in_{name}_dram"] = a
        args.append(nc.dram_tensor(f"in_{name}_dram", a.shape, _mybir.dt.from_np(a.dtype), kind="ExternalInput").ap())
    for i, (shape, dtype) in enumerate(_OUTS):
        dt = _mybir.dt.from_np(_np.dtype(dtype))
        args.append(nc.dram_tensor(f"out_{i}_dram", shape, dt, kind="ExternalOutput").ap())
    vision_layer(nc, *args)
    r = _run(nc, [arrays], core_ids=[0])
    got = tuple(r.results[0][f"out_{i}_dram"] for i in range(len(_OUTS)))
    return got[0]
```
